# Optimizing a Trainium2 kernel written in Bass

```python
import numpy as np
import jax
import jax.numpy as jnp

def _softmax(x, axis=-1):
    return jax.nn.softmax(x, axis=axis)

def _gelu(x):
    return jax.nn.gelu(x, approximate=True)

def _silu(x):
    return jax.nn.silu(x)

def _sigmoid(x):
    return jax.nn.sigmoid(x)

def _layernorm(x, axis=-1, eps=1e-05):
    m = jnp.mean(x, axis=axis, keepdims=True)
    v = jnp.var(x, axis=axis, keepdims=True)
    return (x - m) / jnp.sqrt(v + eps)

def _scatter_add(tgt, idx, src, axis=0):
    return tgt.at[idx].add(src)

def _segment_sum(src, seg, n):
    return jax.ops.segment_sum(src, seg, n)
kernel_name = 'mk_xattn_ffn_d1_seqx_r4_51acaf'

def setup_inputs(seed: int=0):
    np.random.seed(seed)
    _w = jnp.asarray

    def _rec_inputs():
        import jax
        import jax.numpy as jnp
        _rk = jax.random.key(seed)
        x = -0.0002928 + 1 * jax.random.normal(jax.random.fold_in(_rk, 1), (8, 512, 256), jnp.float32)
        _lenS = 512 - jax.random.randint(jax.random.fold_in(_rk, 7), (8,), 0, max(1, 512 // 4) + 1, jnp.int32)
        _lenS2 = 64 - jax.random.randint(jax.random.fold_in(_rk, 8), (8,), 0, max(1, 64 // 4) + 1, jnp.int32)
        _ctx_1024P = jax.random.normal(jax.random.fold_in(_rk, 11), (8, 16, 256), jnp.float32)
        _ctx_1024c = jax.random.dirichlet(jax.random.fold_in(_rk, 511), 0.3 * jnp.ones((16,), jnp.float32), (8, 64))
        _ctx_1024t = jnp.einsum('bsk,bkd->bsd', _ctx_1024c, _ctx_1024P)
        _ctx_1024t = _ctx_1024t * jax.lax.rsqrt(jnp.mean(jnp.square(_ctx_1024t)) + 1e-12) * 0.953939
        ctx_1024 = -1.39393e-06 + 0.999914 * (_ctx_1024t + 0.3 * jax.random.normal(jax.random.fold_in(_rk, 611), (8, 64, 256), jnp.float32))
        _validS = jnp.arange(512)[None, :] < _lenS[:, None]
        _validS2 = jnp.arange(64)[None, :] < _lenS2[:, None]
        _causal = jnp.tril(jnp.ones((512, 512), dtype=bool))
        mask_BxSxS2_ff1 = jnp.where(jnp.ones((8, 512, 64), dtype=bool), 1.0, 0.0).astype(jnp.float32)
        return (x, ctx_1024, mask_BxSxS2_ff1)
    x, ctx_1024, mask_BxSxS2_ff1 = _rec_inputs()

    def _L0_xattn_setup():
        import jax, jax.numpy as jnp
        import numpy as np
        B, S, D, H = (2, 512, 256, 16)
        DK = D // H
        key = jax.random.key(seed)
        ks = jax.random.split(key, 12)
        sc = 1.0 / np.sqrt(D)
        return {'target': jax.random.normal(ks[0], (B, S, D), jnp.float32), 'source': jax.random.normal(ks[1], (B, S, D), jnp.float32), 'memory': jax.random.normal(ks[2], (B, S, D), jnp.float32), 'mask': jnp.ones((B, S, S), jnp.float32), 'WQ': jax.random.normal(ks[3], (D, D), jnp.float32) * sc, 'bQ': jnp.zeros((D,), jnp.float32), 'WK': jax.random.normal(ks[4], (D, D), jnp.float32) * sc, 'bK': jnp.zeros((D,), jnp.float32), 'WV': jax.random.normal(ks[5], (D, D), jnp.float32) * sc, 'bV': jnp.zeros((D,), jnp.float32), 'Wp': jax.random.normal(ks[6], (D, D), jnp.float32) * sc, 'bp': jnp.zeros((D,), jnp.float32)}
    _L0_xattn_all = _L0_xattn_setup()
    _L0_xattn_in = {k: v for k, v in _L0_xattn_all.items() if k in ('WQ', 'bQ', 'WK', 'bK', 'WV', 'bV', 'Wp', 'bp')}
    del _L0_xattn_all

    def _L0_ffn_setup():
        import jax, jax.numpy as jnp
        import numpy as np
        NUM_EXPERTS = 8
        HIDDEN = 256
        D_FF = 1024
        SCALE = 0.8
        SPARSITY = 0.1

        def _perturb_attractive(w, scale=SCALE, sparsity=SPARSITY):
            a = jnp.abs(w)
            flat = a.ravel()
            n = flat.shape[0]
            k = max(1, int(n * sparsity / 2))
            s = jnp.sort(flat)
            thr_bot = s[k - 1]
            thr_top = s[n - k]
            tier = jnp.where(a >= thr_top, -1.0, jnp.where(a <= thr_bot, 1.0, 0.0))
            return w + scale * w * tier

        def _stack_expert_params(w):
            pw = _perturb_attractive(w)
            return jnp.concatenate([w[None], jnp.broadcast_to(pw, (NUM_EXPERTS - 1,) + w.shape)], axis=0)
        key = jax.random.key(seed)
        ks = jax.random.split(key, 6)
        B, S, H, F, E = (2, 512, HIDDEN, D_FF, NUM_EXPERTS)
        return {'x': jax.random.normal(ks[0], (B, S, H), dtype=jnp.float32), 'W1': jax.random.normal(ks[1], (H, F), dtype=jnp.float32) * (1.0 / np.sqrt(H)), 'b1': jax.random.normal(ks[2], (F,), dtype=jnp.float32) * 0.02, 'W2': jax.random.normal(ks[3], (F, H), dtype=jnp.float32) * (1.0 / np.sqrt(F)), 'b2': jax.random.normal(ks[4], (H,), dtype=jnp.float32) * 0.02, 'ln_gamma': jnp.ones((H,), dtype=jnp.float32), 'ln_beta': jnp.zeros((H,), dtype=jnp.float32), 'Wr': jax.random.normal(ks[5], (H, E), dtype=jnp.float32) * (1.0 / np.sqrt(H)), 'br': jnp.zeros((E,), dtype=jnp.float32)}
    _L0_ffn_all = _L0_ffn_setup()
    _L0_ffn_in = {k: v for k, v in _L0_ffn_all.items() if k in ('W1', 'b1', 'W2', 'b2', 'ln_gamma', 'ln_beta', 'Wr', 'br')}
    del _L0_ffn_all
    return {'x': x, 'ctx_1024': ctx_1024, 'mask_BxSxS2_ff1': mask_BxSxS2_ff1, 'L0_xattn_WQ': _L0_xattn_in['WQ'], 'L0_xattn_bQ': _L0_xattn_in['bQ'], 'L0_xattn_WK': _L0_xattn_in['WK'], 'L0_xattn_bK': _L0_xattn_in['bK'], 'L0_xattn_WV': _L0_xattn_in['WV'], 'L0_xattn_bV': _L0_xattn_in['bV'], 'L0_xattn_Wp': _L0_xattn_in['Wp'], 'L0_xattn_bp': _L0_xattn_in['bp'], 'L0_ffn_W1': _L0_ffn_in['W1'], 'L0_ffn_b1': _L0_ffn_in['b1'], 'L0_ffn_W2': _L0_ffn_in['W2'], 'L0_ffn_b2': _L0_ffn_in['b2'], 'L0_ffn_ln_gamma': _L0_ffn_in['ln_gamma'], 'L0_ffn_ln_beta': _L0_ffn_in['ln_beta'], 'L0_ffn_Wr': _L0_ffn_in['Wr'], 'L0_ffn_br': _L0_ffn_in['br']}

def reference(x, ctx_1024, mask_BxSxS2_ff1, L0_xattn_WQ, L0_xattn_bQ, L0_xattn_WK, L0_xattn_bK, L0_xattn_WV, L0_xattn_bV, L0_xattn_Wp, L0_xattn_bp, L0_ffn_W1, L0_ffn_b1, L0_ffn_W2, L0_ffn_b2, L0_ffn_ln_gamma, L0_ffn_ln_beta, L0_ffn_Wr, L0_ffn_br):
    import jax
    import jax.numpy as jnp

    def _L0_xattn_ref(target, source, memory, mask, WQ, bQ, WK, bK, WV, bV, Wp, bp):
        import jax, jax.numpy as jnp
        import numpy as np
        B, S, D, H = (2, 512, 256, 16)
        DK = D // H
        b = target.shape[0]
        Q = (target @ WQ + bQ).reshape(b, H, -1, DK)
        K = (source @ WK + bK).reshape(b, H, -1, DK)
        V = (memory @ WV + bV).reshape(b, H, -1, DK)
        scale = jnp.asarray(K.shape[-1], jnp.float32) ** 0.5
        QK_T = jnp.einsum('bhqd,bhkd->bhqk', Q, K)
        QK_T = QK_T * mask[:, None, :, :]
        attn = jax.nn.softmax(QK_T, axis=-1) / scale
        out = jnp.einsum('bhqk,bhkd->bhqd', attn, V)
        out = out.transpose(0, 2, 1, 3).reshape(b, -1, D)
        return out @ Wp + bp

    def _L0_ffn_ref(x, W1, b1, W2, b2, ln_gamma, ln_beta, Wr, br):
        import jax, jax.numpy as jnp
        import numpy as np
        NUM_EXPERTS = 8
        HIDDEN = 256
        D_FF = 1024
        SCALE = 0.8
        SPARSITY = 0.1

        def _perturb_attractive(w, scale=SCALE, sparsity=SPARSITY):
            a = jnp.abs(w)
            flat = a.ravel()
            n = flat.shape[0]
            k = max(1, int(n * sparsity / 2))
            s = jnp.sort(flat)
            thr_bot = s[k - 1]
            thr_top = s[n - k]
            tier = jnp.where(a >= thr_top, -1.0, jnp.where(a <= thr_bot, 1.0, 0.0))
            return w + scale * w * tier

        def _stack_expert_params(w):
            pw = _perturb_attractive(w)
            return jnp.concatenate([w[None], jnp.broadcast_to(pw, (NUM_EXPERTS - 1,) + w.shape)], axis=0)
        mu = jnp.mean(x, axis=-1, keepdims=True)
        var = jnp.mean(jnp.square(x - mu), axis=-1, keepdims=True)
        h = (x - mu) * jax.lax.rsqrt(var + 1e-05) * ln_gamma + ln_beta
        logits = jnp.einsum('bsh,he->bse', h, Wr) + br
        probs = jax.nn.softmax(logits, axis=-1)
        W1s = _stack_expert_params(W1)
        b1s = _stack_expert_params(b1)
        W2s = _stack_expert_params(W2)
        b2s = _stack_expert_params(b2)
        pre = jnp.einsum('bsh,ehf->besf', x, W1s) + b1s[None, :, None, :]
        act = jax.nn.gelu(pre)
        y = jnp.einsum('besf,efh->besh', act, W2s) + b2s[None, :, None, :]
        out = jnp.einsum('bse,besh->bsh', probs, y)
        return out
    x = x + _L0_xattn_ref(_layernorm(x, axis=-1), ctx_1024, ctx_1024, mask_BxSxS2_ff1, L0_xattn_WQ, L0_xattn_bQ, L0_xattn_WK, L0_xattn_bK, L0_xattn_WV, L0_xattn_bV, L0_xattn_Wp, L0_xattn_bp)
    x = x + _L0_ffn_ref(_layernorm(x, axis=-1), L0_ffn_W1, L0_ffn_b1, L0_ffn_W2, L0_ffn_b2, L0_ffn_ln_gamma, L0_ffn_ln_beta, L0_ffn_Wr, L0_ffn_br)
    return x

_drawn_inputs = setup_inputs


def setup_inputs(seed=0):
    import zlib

    import numpy as np

    out = dict(_drawn_inputs(seed))
    spreads = {'L0_xattn_bQ': (0.0, 0.1),
     'L0_xattn_bK': (0.0, 0.1),
     'L0_xattn_bV': (0.0, 0.442),
     'L0_xattn_bp': (0.0, 0.1),
     'L0_ffn_ln_gamma': (1.0, 0.6),
     'L0_ffn_ln_beta': (0.0, 0.8),
     'L0_ffn_br': (0.0, 0.8)}
    factors = {'L0_ffn_b1': 6.481, 'L0_ffn_b2': 3.768}
    for name, (base, spread) in spreads.items():
        noise = np.random.default_rng([zlib.crc32(name.encode()), seed]).standard_normal(out[name].shape)
        drawn = base * np.exp(spread * noise) if base else spread * noise
        out[name] = jnp.asarray(drawn.astype(out[name].dtype))
    for name, factor in factors.items():
        out[name] = (out[name] * factor).astype(out[name].dtype)
    return out
```

```python
from contextlib import ExitStack

import concourse.bass as bass
from concourse import mybir

ALU = mybir.AluOpType
ACT = mybir.ActivationFunctionType
AX = mybir.AxisListType
F32 = mybir.dt.float32
F32R = mybir.dt.float32r
BF16 = mybir.dt.bfloat16
U16 = mybir.dt.uint16
U32 = mybir.dt.uint32

P = 128
EPS = 1e-5
SPARSITY = 0.1
SCALE = 0.8
BITS = 16


class Signal:

    def __init__(self, handle, per):
        self.handle, self.per = handle, per

    def at(self, batch, count=None):
        return (batch + 1) * self.per + (self.per if count is None else count)


def build_program(nc, x, ctx_in, mask, WQ, bQ, WK, bK, WV, bV, Wp, bp,
                  W1, b1, W2, b2, gamma, beta, Wr, br, out):
    B, S, D = x.shape
    CT = ctx_in.shape[1]
    F = W1.shape[1]
    E = Wr.shape[1]
    H = 16
    DK = D // H
    NT = S // P
    DC = D // P
    FC = F // P
    HH = H // 2
    R = S // H
    C = S // R
    G = H // 2
    VW = 2 * DK + 2
    KC = B * CT // P
    assert (P, DC, R * C, HH * DK, 2 * CT, HH * CT) == (128, 2, S, P, P, 512)

    def rank(n, top):
        k = max(1, int(n * SPARSITY / 2))
        return n - k + 1 if top else k
    SEARCH_N = [D * F, D * F, D * F, D * F, F, F, D, D]
    RANKS = [rank(n, s % 2 == 0) for s, n in enumerate(SEARCH_N)]
    NS = len(RANKS)
    WN = D * F // P

    ctx = ExitStack()

    def sb(name, shape, dt=F32):
        return ctx.enter_context(nc.sbuf_tensor(name, shape, dt))

    def sig(name, per=1):
        s = Signal(ctx.enter_context(nc.semaphore(name)), per)
        signals.append(s)
        return s

    def sem(name):
        return ctx.enter_context(nc.semaphore(name))

    signals = []

    ps_s = ctx.enter_context(nc.psum_tensor("ps_s", [P, 2, 512], F32))
    ps_l = ctx.enter_context(nc.psum_tensor("ps_l", [P, 2, 512], F32))
    ps_y = ctx.enter_context(nc.psum_tensor("ps_y", [P, 2, 512], F32))
    ps_m = ctx.enter_context(nc.psum_tensor("ps_m", [P, 2, 512], F32))

    q_scr = nc.dram_tensor("q_scr", [B, D, S], F32, kind="Internal").ap()
    v_scr = nc.dram_tensor("v_scr", [B, CT, D], F32, kind="Internal").ap()
    k_scr = nc.dram_tensor("k_scr", [B, CT, D], F32, kind="Internal").ap()
    kh_scr = nc.dram_tensor("kh_scr", [2, P, DC * B * CT], F32, kind="Internal").ap()
    xt_scr = nc.dram_tensor("xt_scr", [B, P, DC * S], F32, kind="Internal").ap()
    acc_scr = nc.dram_tensor("acc_scr", [B, P, NT * (D + 1)], F32, kind="Internal").ap()

    def view(region, start, *shape):
        n = 1
        for d in shape:
            n *= d
        ap = region[:, start:start + n]
        names = "abc"[:len(shape)]
        if len(shape) == 1:
            return ap
        return ap.rearrange("p (" + " ".join(names) + ") -> p " + " ".join(names), **dict(zip(names[1:], shape[1:])))

    region_a = sb("region_a", [P, 6 * H * CT])
    region_b = sb("region_b", [P, 2 * WN])
    region_c = [sb(f"region_c_{n}", [P, 4 * S], F32R) for n in ("hi", "lo")]
    stage = view(region_a, 0, 4 * DC * D)
    ctxt = view(region_a, 4 * DC * D, KC, D)
    kv = view(region_a, 4 * DC * D + KC * D, 2, KC, D)
    kk = view(region_a, 4 * DC * D + 3 * KC * D, KC, D)
    sc = view(region_a, 0, 2, H * CT)
    pr = view(region_a, 2 * H * CT, 2, H * CT)
    pT = view(region_a, 4 * H * CT, 2, G * P)
    wraw = view(region_b, 0, 2, WN)
    x2T = view(region_b, 0, DC, S)
    yT = view(region_b, DC * S, DC, S)
    g = view(region_b, 2 * DC * S, 4, S)
    wagain = view(region_a, 0, 2, WN)
    tier = view(region_a, 2 * WN, WN)
    cT = [view(r, 0, DC, B * CT) for r in region_c]
    kT = [view(r, DC * B * CT, DC, B * CT) for r in region_c]
    gs = [view(r, 0, 4, S) for r in region_c]

    ident = sb("ident", [P, P])
    ones = sb("ones", [P, P])
    ones_bf = sb("ones_bf", [P, 2], BF16)
    mhalf = sb("mhalf", [P, NT])
    wqkvp = [sb(f"wqkvp_{n}", [P, 4, DC, D], F32R) for n in ("hi", "lo")]
    bq = sb("bq", [P, DC])
    rows = sb("rows", [P, 3, D])
    bkb, bvb, bpb = (rows[:, n, :] for n in range(3))
    w1s = [sb(f"w1_{n}", [P, DC * F], F32R) for n in ("hi", "lo")]
    w2s = [sb(f"w2_{n}", [P, FC * D], F32R) for n in ("hi", "lo")]
    bias = sb("bias", [P, 2, FC + DC])
    gam = sb("gam", [P, DC])
    bet = sb("bet", [P, DC])
    wr = sb("wr", [P, DC, E])
    gw = sb("gw", [P, DC, E])
    bw = sb("bw", [P, DC, E])
    brb = sb("brb", [P, E])
    rc = sb("rc", [P, 2, E])

    key = sb("key", [P, 4, WN], U16)
    skey = sb("skey", [P, 2 * (FC + DC)], U16)
    ind = [sb(f"ind{n}", [P, WN], BF16) for n in range(2)]
    sind = sb("sind", [P, 2 * (FC + DC)], BF16)
    sabs = sb("sabs", [P, FC + DC])
    ranks = sb("ranks", [P, NS])
    prefix = sb("prefix", [P, NS])
    cand = sb("cand", [P, NS])
    half = sb("half", [P, 1])
    below = sb("below", [P, NS])
    cnt = sb("cnt", [P, NS])
    fail = sb("fail", [P, NS])
    fcnt = sb("fcnt", [P, NS])
    thr = sb("thr", [P, NS, 2], U16)

    xa = sb("xa", [P, NT, D])
    xr = sb("xr", [P, NT, D])
    mk = sb("mk", [P, NT, CT])
    stat = sb("stat", [P, NT, 6])
    mv = sb("mv", [P, NT, 2])
    var = sb("var", [P, NT])
    carry = sb("carry", [P, 1])
    rstd = sb("rstd", [P, NT])
    xh = sb("xh", [P, NT, D])
    xhT = [sb(f"xhT_{n}", [P, DC, S], F32R) for n in ("hi", "lo")]
    qf = sb("qf", [P, DC, S])
    qr = sb("qr", [P, DC, S])
    qs = [sb(f"qs_{n}", [P, DC, S], F32R) for n in ("hi", "lo")]
    kbd = [sb(f"kbd_{n}", [P, DC, HH, CT], F32R) for n in ("hi", "lo")]
    vbd = sb("vbd", [P, G, VW])
    mx = sb("mx", [P, 2, H])
    rs = sb("rs", [P, 2, H])
    on = sb("on", [P, NT, D])
    oT = xhT
    x2 = sb("x2", [P, NT, D])

    x2s = [sb(f"x2s_{n}", [P, DC, S], F32R) for n in ("hi", "lo")]
    nm = sb("nm", [P, NT])
    lg = sb("lg", [P, NT, E])
    lt = sb("lt", [P, NT, E])
    lmx = sb("lmx", [P, NT])
    s8 = sb("s8", [P, NT])
    s7 = sb("s7", [P, NT])
    p0 = sb("p0", [P, NT])
    acc = sb("acc", [P, NT, D + 1])

    ld_small = sem("ld_small")
    ld_ctx = sem("ld_ctx")
    ld_w = sem("ld_w")
    ld_again = sem("ld_again")
    consts_ready = sem("consts_ready")
    eye_ready = sem("eye_ready")
    proj_hi = sem("proj_hi")
    proj_lo = sem("proj_lo")
    ctx_turned = sem("ctx_turned")
    ctx_hi = sem("ctx_hi")
    ctx_lo = sem("ctx_lo")
    kv_product = sem("kv_product")
    kv_biased = sem("kv_biased")
    kv_out = sem("kv_out")
    kk_in = sem("kk_in")
    k_turned = sem("k_turned")
    k_hi = sem("k_hi")
    k_lo = sem("k_lo")
    kh_out = sem("kh_out")
    w_hi = sem("w_hi")
    w_lo = sem("w_lo")
    route_w = sem("route_w")
    route_sum = sem("route_sum")
    route_ready = sem("route_ready")
    mag_ready = sem("mag_ready")
    key_ready = sem("key_ready")
    state_ready = sem("state_ready")
    key_mark = sem("key_mark")
    thr_ready = sem("thr_ready")
    tier_step = sem("tier_step")
    pw_ready = sem("pw_ready")
    pw_hi = sem("pw_hi")
    pw_lo = sem("pw_lo")
    pb_ready = sem("pb_ready")

    ind_ready = sig("ind_ready", 4)
    ind_counted = sig("ind_counted", 4)
    cnt_ready = sig("cnt_ready", 5)
    total_ready = sig("total_ready")
    failed = sig("failed")
    below_step = sig("below_step")
    prefix_step = sig("prefix_step", 2)
    cand_step = sig("cand_step")

    x_in = sig("x_in", 16)
    xr_in = sig("xr_in", 16 * NT)
    mask_in = sig("mask_in", 16 * NT)
    v_in = sig("v_in", 32)
    k_in = sig("k_in", 16 * 2 * HH)
    q_out = sig("q_out", 16)
    q_in = sig("q_in", 16 * H)
    ln = [dict(stats=sig(f"ln{n}_stats", NT), mean=sig(f"ln{n}_mean", NT), var=sig(f"ln{n}_var"),
               rstd=sig(f"ln{n}_rstd"), xhat=sig(f"ln{n}_xhat", NT)) for n in range(3)]
    xT_turned = sig("xT_turned")
    xT_hi = sig("xT_hi")
    xT_lo = sig("xT_lo")
    q_product = sig("q_product", DC)
    q_biased = sig("q_biased", DC)
    q_hi = sig("q_hi")
    q_lo = sig("q_lo")
    s_product = sig("s_product", NT)
    s_masked = sig("s_masked", NT)
    s_max = sig("s_max", NT)
    s_shifted = sig("s_shifted", NT)
    p_exp = sig("p_exp", NT)
    p_turned = sig("p_turned", NT)
    pT_ready = sig("pT_ready", NT)
    o_product = sig("o_product", NT)
    o_recip = sig("o_recip", NT)
    o_norm = sig("o_norm", NT)
    o_turned = sig("o_turned")
    oT_hi = sig("oT_hi")
    oT_lo = sig("oT_lo")
    a_product = sig("a_product", 2)
    xr_biased = sig("xr_biased")
    x2_ready = sig("x2_ready", 2)
    x2_turned = sig("x2_turned")
    x2T_ready = sig("x2T_ready")
    x2T_out = sig("x2T_out", 16)
    r_product = sig("r_product")
    r_step = sig("r_step", 7)
    r_exp = sig("r_exp")
    r_sum = sig("r_sum", 3)
    r_probs = sig("r_probs", 2)

    ex = [dict(
        x2_hi=sig(f"e{e}_x2_hi"), x2_lo=sig(f"e{e}_x2_lo"),
        h_product=sig(f"e{e}_h_product", FC), gelu=sig(f"e{e}_gelu", FC),
        g_hi=sig(f"e{e}_g_hi", FC), g_lo=sig(f"e{e}_g_lo", FC),
        y_step=sig(f"e{e}_y_step", FC), y_biased=sig(f"e{e}_y_biased", DC),
        y_turned=sig(f"e{e}_y_turned"), mixed=sig(f"e{e}_mixed", NT),
        acc_io=sig(f"e{e}_acc_io", 16), out_io=sig(f"e{e}_out_io", 16 * NT)) for e in range(2)]
    xt_in = sig("xt_in", 16)

    def perm(ap):
        return ap.rearrange("(r c) d -> c r d", c=C)

    def three(eng, out_ap, a, b, first=True, last=True):
        eng.matmul(out_ap, a[0], b[0], start=first, stop=False)
        eng.matmul(out_ap, a[0], b[1], start=False, stop=False)
        return eng.matmul(out_ap, a[1], b[0], start=False, stop=last)

    with nc.Block() as credit:
        @credit.gpsimd
        def _(pool):
            for s in signals:
                pool.sem_inc(s.handle, s.per)

    block = ctx.enter_context(nc.Block())

    @block.sync
    def _(sp):
        with nc.allow_non_contiguous_dma(reason="small vectors laid out by partition"):
            for n, w in enumerate((WQ, WK, WV, Wp)):
                sp.dma_start(view(region_a, n * DC * D, DC, D), w.rearrange("(c p) n -> p c n", p=P)).then_inc(ld_small, 16)
            for n, v in enumerate((bK, bV, bp)):
                sp.dma_start(rows[:, n, :], v.rearrange("(a d) -> a d", a=1).to_broadcast([P, D])).then_inc(ld_small, 16)
            for k in range(KC):
                sp.dma_start(ctxt[:, k, :], ctx_in.rearrange("b t d -> (b t) d")[k * P:(k + 1) * P]).then_inc(ld_ctx, 16)
            sp.dma_start(bq[:], bQ.rearrange("(c p) -> p c", p=P)).then_inc(ld_small, 16)
            sp.dma_start(wraw[:, 0].rearrange("p (c f) -> p c f", c=DC), W1.rearrange("(c p) f -> p c f", p=P)).then_inc(ld_w, 16)
            sp.dma_start(wraw[:, 1].rearrange("p (c d) -> p c d", c=FC), W2.rearrange("(c p) d -> p c d", p=P)).then_inc(ld_w, 16)
            sp.dma_start(bias[:, 0, 0:FC], b1.rearrange("(c p) -> p c", p=P)).then_inc(ld_w, 16)
            sp.dma_start(bias[:, 0, FC:FC + DC], b2.rearrange("(c p) -> p c", p=P)).then_inc(ld_w, 16)
            sp.dma_start(gam[:], gamma.rearrange("(c p) -> p c", p=P)).then_inc(ld_small, 16)
            sp.dma_start(bet[:], beta.rearrange("(c p) -> p c", p=P)).then_inc(ld_small, 16)
            sp.dma_start(wr[:], Wr.rearrange("(c p) e -> p c e", p=P)).then_inc(ld_small, 16)
            sp.dma_start(brb[:], br.rearrange("(a e) -> a e", a=1).to_broadcast([P, E])).then_inc(ld_small, 16)
        sp.wait_ge(kv_biased, 2 * KC)
        sp.dma_start(k_scr.rearrange("b t d -> (b t) d").rearrange("(k p) d -> p k d", p=P), kv[:, 0]).then_inc(kv_out, 16)
        sp.dma_start(v_scr.rearrange("b t d -> (b t) d").rearrange("(k p) d -> p k d", p=P), kv[:, 1]).then_inc(kv_out, 16)
        sp.wait_ge(kv_out, 32)
        for b in range(B):
            sp.dma_start(kk[CT * (b % 2):CT * (b % 2) + CT, b // 2].rearrange("k (h d) -> k h d", d=DK),
                         k_scr[b].rearrange("t (c d) -> (t c) d", d=DK).rearrange("(h k) d -> k h d", k=CT)).then_inc(kk_in, 16)
        sp.wait_ge(k_lo, 1)
        for n in range(2):
            sp.dma_start(kh_scr[n], kT[n].rearrange("p c k -> p (c k)").bitcast(F32)).then_inc(kh_out, 16)
        sp.wait_ge(kh_out, 32)

        sp.wait_ge(eye_ready, 6)

        def attention(b):
            sp.wait_ge(ln[0]["xhat"].handle, ln[0]["xhat"].at(b - 1))
            sp.dma_start(xa[:], x[b].rearrange("(t p) d -> p t d", p=P)).then_inc(x_in.handle, 16)
            sp.wait_ge(s_masked.handle, s_masked.at(b - 1))
            for j in range(NT):
                sp.dma_start(mk[:, j, :], perm(mask[b])[4 * j:4 * j + 4]).then_inc(mask_in.handle, 16)
            sp.wait_ge(s_product.handle, s_product.at(b - 1))
            for h in range(HH):
                for n in range(2):
                    sp.dma_start(kbd[n][DK * h:DK * h + DK, :, h, :].bitcast(F32),
                                 kh_scr[n, DK * h:DK * h + DK].rearrange("p (c b k) -> b p c k", k=CT, c=DC)[b]).then_inc(k_in.handle, 16)
            sp.wait_ge(o_product.handle, o_product.at(b - 1))
            for o in range(2):
                sp.dma_start(vbd[CT * o:CT * o + CT, :, DK * o:DK * o + DK],
                             v_scr[b].rearrange("t (c d) -> (t c) d", d=DK).rearrange("(g o k) d -> o k g d", k=CT, o=2)[o]).then_inc(v_in.handle, 16)
            sp.wait_ge(q_biased.handle, q_biased.at(b))
            sp.dma_start(q_scr[b].rearrange("(m p) s -> p m s", p=P), qf[:]).then_inc(q_out.handle, 16)
            sp.wait_ge(q_out.handle, q_out.at(b))
            for h in range(H):
                sp.dma_start(qr[DK * (h % HH):DK * (h % HH) + DK, h // HH].rearrange("p (c r) -> p c r", r=R),
                             q_scr[b].rearrange("(c d) (h r) -> h d c r", d=DK, r=R)[h]).then_inc(q_in.handle, 16)
            sp.wait_ge(x2_ready.handle, x2_ready.at(b - 1))
            for j in range(NT):
                sp.dma_start(xr[:, j, :], perm(x[b])[4 * j:4 * j + 4]).then_inc(xr_in.handle, 16)
            sp.wait_ge(x2T_ready.handle, x2T_ready.at(b))
            sp.dma_start(xt_scr[b], x2T.rearrange("p c s -> p (c s)")).then_inc(x2T_out.handle, 16)

        with sp.Fori(0, B) as b:
            attention(b)
            m = ex[0]["mixed"]
            sp.wait_ge(m.handle, m.at(b))
            sp.dma_start(acc_scr[b], acc[:].rearrange("p t d -> p (t d)")).then_inc(ex[0]["acc_io"].handle, 16)
        sp.wait_ge(x2T_out.handle, x2T_out.at(B - 1))
        sp.wait_ge(ex[0]["acc_io"].handle, ex[0]["acc_io"].at(B - 1))
        sp.wait_ge(o_product.handle, o_product.at(B - 1))
        sp.dma_start(wagain[:, 0].rearrange("p (c f) -> p c f", c=DC), W1.rearrange("(c p) f -> p c f", p=P)).then_inc(ld_again, 16)
        sp.dma_start(wagain[:, 1].rearrange("p (c d) -> p c d", c=FC), W2.rearrange("(c p) d -> p c d", p=P)).then_inc(ld_again, 16)
        with sp.Fori(0, B) as b:
            sp.wait_ge(ex[1]["x2_lo"].handle, ex[1]["x2_lo"].at(b - 1))
            sp.dma_start(x2T.rearrange("p c s -> p (c s)"), xt_scr[b]).then_inc(xt_in.handle, 16)
            m = ex[1]["out_io"]
            sp.wait_ge(m.handle, m.at(b - 1))
            sp.dma_start(acc[:].rearrange("p t d -> p (t d)"), acc_scr[b]).then_inc(ex[1]["acc_io"].handle, 16)
            sp.wait_ge(ex[1]["mixed"].handle, ex[1]["mixed"].at(b))
            for j in range(NT):
                sp.dma_start(perm(out[b])[4 * j:4 * j + 4], acc[:, j, 0:D]).then_inc(m.handle, 16)
        sp.wait_ge(ex[1]["out_io"].handle, ex[1]["out_io"].at(B - 1))

    @block.tensor
    def _(pe):
        def w_of(n, c, cols):
            return [w[:, n, c, cols] for w in wqkvp]

        pe.wait_ge(ld_ctx, 16 * KC)
        pe.wait_ge(eye_ready, 1)
        for c in range(DC):
            for k in range(KC):
                mm = pe.transpose(ps_m[:, c, k * P:(k + 1) * P], ctxt[:, k, c * P:(c + 1) * P], ident[:])
        mm.then_inc(ctx_turned, 1)
        pe.wait_ge(proj_lo, 1)
        pe.wait_ge(ctx_lo, 1)
        for n, dst in ((1, ps_s), (2, ps_y)):
            for k in range(KC):
                for c in range(DC):
                    mm = three(pe, dst[:, k // 2, (k % 2) * D:(k % 2) * D + D],
                               [t[:, c, k * P:(k + 1) * P] for t in cT], w_of(n, c, slice(0, D)),
                               c == 0, c == DC - 1)
                mm.then_inc(kv_product, 1)
        pe.wait_ge(kk_in, 16 * B)
        pe.wait_ge(kv_biased, KC)
        for c in range(DC):
            for k in range(KC):
                mm = pe.transpose(ps_l[:, c, k * P:(k + 1) * P], kk[:, k, c * P:(c + 1) * P], ident[:])
        mm.then_inc(k_turned, 1)
        pe.wait_ge(consts_ready, 4)
        pe.wait_ge(route_w, 2 * DC)
        for n, w in enumerate((gw, bw)):
            for c in range(DC):
                mm = pe.matmul(ps_m[:, 0, n * E:(n + 1) * E], ones[:], w[:, c, :], start=c == 0, stop=c == DC - 1)
        mm.then_inc(route_sum, 1)
        pe.wait_ge(route_ready, 1)

        def search_step(i):
            for s in range(4):
                pe.wait_ge(ind_ready.handle, ind_ready.at(i, s + 1))
                if s == 0:
                    pe.wait_ge(cnt_ready.handle, cnt_ready.at(i - 1))
                for c in range(WN // P):
                    mm = pe.matmul(ps_s[:, 0, s:s + 1], ind[s % 2][:, c * P:(c + 1) * P], ones_bf[:, 0:1],
                                   start=c == 0, stop=c == WN // P - 1)
                mm.then_inc(ind_counted.handle, 1)
            pe.wait_ge(cnt_ready.handle, cnt_ready.at(i))
            pe.wait_ge(below_step.handle, below_step.at(i - 1))
            pe.matmul(ps_s[:, 1, 0:NS], ones[:], cnt[:], start=True, stop=True).then_inc(total_ready.handle, 1)

        with pe.Fori(0, BITS) as i:
            search_step(i)
        with pe.Fori(BITS, 2 * BITS) as i:
            search_step(i)

        def attention(b):
            pe.wait_ge(ln[0]["xhat"].handle, ln[0]["xhat"].at(b))
            pe.wait_ge(ex[0]["mixed"].handle, ex[0]["mixed"].at(b - 1))
            for c in range(DC):
                for t in range(NT):
                    mm = pe.transpose(ps_m[:, c, t * P:(t + 1) * P], xh[:, t, c * P:(c + 1) * P], ident[:])
            mm.then_inc(xT_turned.handle, 1)
            pe.wait_ge(xT_hi.handle, xT_hi.at(b))
            pe.wait_ge(xT_lo.handle, xT_lo.at(b))
            pe.wait_ge(ex[0]["gelu"].handle, ex[0]["gelu"].at(b - 1))
            for m in range(DC):
                for c in range(DC):
                    mm = three(pe, ps_l[:, m, :], w_of(0, c, slice(m * P, (m + 1) * P)),
                               [t[:, c, :] for t in xhT], c == 0, c == DC - 1)
                mm.then_inc(q_product.handle, 1)

            def scores(j):
                if j == 0:
                    pe.wait_ge(q_hi.handle, q_hi.at(b))
                    pe.wait_ge(q_lo.handle, q_lo.at(b))
                    pe.wait_ge(k_in.handle, k_in.at(b))
                else:
                    pe.wait_ge(s_masked.handle, s_masked.at(b, j))
                for m in range(DC):
                    mm = three(pe, ps_s[:, m, :], [t[:, m, j * P:(j + 1) * P] for t in qs],
                               [t[:, m].rearrange("p h k -> p (h k)") for t in kbd])
                mm.then_inc(s_product.handle, 1)

            def turn_probs(j):
                pe.wait_ge(p_exp.handle, p_exp.at(b, j + 1))
                if j == 0:
                    pe.wait_ge(q_biased.handle, q_biased.at(b))
                else:
                    pe.wait_ge(pT_ready.handle, pT_ready.at(b, j))
                for n in range(G):
                    mm = pe.transpose(ps_l[:, n // 4, (n % 4) * P:(n % 4 + 1) * P], pr[:, j % 2, n * P:(n + 1) * P], ident[:])
                mm.then_inc(p_turned.handle, 1)

            def values(j):
                pe.wait_ge(pT_ready.handle, pT_ready.at(b, j + 1))
                if j == 0:
                    pe.wait_ge(v_in.handle, v_in.at(b))
                if j >= 2:
                    pe.wait_ge(o_norm.handle, o_norm.at(b, j - 1))
                for n in range(G):
                    mm = pe.matmul(ps_m[:, j % 2, n * VW:(n + 1) * VW], pT[:, j % 2, n * P:(n + 1) * P], vbd[:, n, :],
                                   start=True, stop=True)
                mm.then_inc(o_product.handle, 1)

            scores(0)
            for j in range(NT):
                if j + 1 < NT:
                    scores(j + 1)
                turn_probs(j)
                if j >= 1:
                    values(j - 1)
            values(NT - 1)
            pe.wait_ge(o_norm.handle, o_norm.at(b))
            pe.wait_ge(s_masked.handle, s_masked.at(b))
            for c in range(DC):
                for t in range(NT):
                    mm = pe.transpose(ps_s[:, c, t * P:(t + 1) * P], on[:, t, c * P:(c + 1) * P], ident[:])
            mm.then_inc(o_turned.handle, 1)
            pe.wait_ge(oT_hi.handle, oT_hi.at(b))
            pe.wait_ge(oT_lo.handle, oT_lo.at(b))
            for t in range(NT):
                for c in range(DC):
                    mm = three(pe, ps_m[:, t // 2, (t % 2) * D:(t % 2) * D + D],
                               [o[:, c, t * P:(t + 1) * P] for o in oT], w_of(3, c, slice(0, D)), c == 0, c == DC - 1)
                if t % 2:
                    mm.then_inc(a_product.handle, 1)
            pe.wait_ge(ln[1]["xhat"].handle, ln[1]["xhat"].at(b))
            for c in range(DC):
                for t in range(NT):
                    mm = pe.transpose(ps_s[:, c, t * P:(t + 1) * P], xh[:, t, c * P:(c + 1) * P], ident[:])
            mm.then_inc(x2_turned.handle, 1)
            pe.wait_ge(x2T_ready.handle, x2T_ready.at(b))
            pe.wait_ge(x2_ready.handle, x2_ready.at(b))
            for t in range(NT):
                for c in range(DC):
                    mm = pe.matmul(ps_m[:, 0, t * E:(t + 1) * E], x2T[:, c, t * P:(t + 1) * P], gw[:, c, :],
                                   start=c == 0, stop=c == DC - 1)
            mm.then_inc(r_product.handle, 1)

        def expert(e, b):
            s = ex[e]
            pe.wait_ge(s["x2_hi"].handle, s["x2_hi"].at(b))
            pe.wait_ge(s["x2_lo"].handle, s["x2_lo"].at(b))

            def hidden(f):
                if f >= 2:
                    pe.wait_ge(s["gelu"].handle, s["gelu"].at(b, f - 1))
                elif e == 1:
                    pe.wait_ge(s["gelu"].handle, s["gelu"].at(b - 1))
                else:
                    pe.wait_ge(pT_ready.handle, pT_ready.at(b))
                for c in range(DC):
                    mm = three(pe, ps_l[:, f % 2, :], [w[:, c * F + f * P:c * F + (f + 1) * P] for w in w1s],
                               [t[:, c, :] for t in x2s], c == 0, c == DC - 1)
                mm.then_inc(s["h_product"].handle, 1)

            def output(f):
                if f == 0:
                    pe.wait_ge(s["y_biased"].handle, s["y_biased"].at(b - 1))
                pe.wait_ge(s["g_hi"].handle, s["g_hi"].at(b, f + 1))
                pe.wait_ge(s["g_lo"].handle, s["g_lo"].at(b, f + 1))
                for m in range(DC):
                    mm = three(pe, ps_y[:, m, :], [w[:, f * D + m * P:f * D + (m + 1) * P] for w in w2s],
                               [t[:, f % 4, :] for t in gs], f == 0, f == FC - 1)
                mm.then_inc(s["y_step"].handle, 1)

            for f in range(FC):
                hidden(f)
                if f >= 3:
                    output(f - 3)
            for f in range(FC - 3, FC):
                output(f)
            pe.wait_ge(s["y_biased"].handle, s["y_biased"].at(b))
            if e == 0:
                pe.wait_ge(r_step.handle, r_step.at(b, 1))
            else:
                pe.wait_ge(s["mixed"].handle, s["mixed"].at(b - 1))
            for t in range(NT):
                for c in range(DC):
                    mm = pe.transpose(ps_m[:, t // 2, (t % 2) * D + c * P:(t % 2) * D + (c + 1) * P],
                                      yT[:, c, t * P:(t + 1) * P], ident[:])
            mm.then_inc(s["y_turned"].handle, 1)

        pe.wait_ge(w_lo, 2)
        with pe.Fori(0, B) as b:
            attention(b)
            expert(0, b)
        pe.wait_ge(ex[0]["mixed"].handle, ex[0]["mixed"].at(B - 1))
        pe.wait_ge(pw_lo, 2)
        with pe.Fori(0, B) as b:
            expert(1, b)

    @block.scalar
    def _(act):
        act.wait_ge(ctx_turned, 1)
        act.activation(cT[0][:], ps_m[:], ACT.Copy).then_inc(ctx_hi, 1)
        act.wait_ge(k_turned, 1)
        act.activation(kT[0][:], ps_l[:], ACT.Copy).then_inc(k_hi, 1)

        def attention(b):
            act.wait_ge(xT_turned.handle, xT_turned.at(b))
            act.wait_ge(q_product.handle, q_product.at(b - 1))
            act.activation(xhT[0][:], ps_m[:], ACT.Copy).then_inc(xT_hi.handle, 1)
            for m in range(DC):
                act.wait_ge(q_product.handle, q_product.at(b, m + 1))
                if m == 0:
                    act.wait_ge(q_out.handle, q_out.at(b - 1))
                act.activation(qf[:, m, :], ps_l[:, m, :], ACT.Identity, bias=bq[:, m:m + 1]).then_inc(q_biased.handle, 1)

            def probs(j):
                act.wait_ge(s_shifted.handle, s_shifted.at(b, j + 1))
                act.wait_ge(p_turned.handle, p_turned.at(b, j - 1) if j >= 2 else p_turned.at(b - 1))
                act.activation(pr[:, j % 2, :], sc[:, j % 2, :], ACT.Exp).then_inc(p_exp.handle, 1)

            def turned(j):
                act.wait_ge(p_turned.handle, p_turned.at(b, j + 1))
                act.wait_ge(o_product.handle, o_product.at(b, j - 1) if j >= 2 else o_product.at(b - 1))
                act.activation(pT[:, j % 2, :], ps_l[:].rearrange("p a b -> p (a b)"), ACT.Copy).then_inc(pT_ready.handle, 1)

            probs(0)
            for j in range(NT):
                if j + 1 < NT:
                    probs(j + 1)
                turned(j)
            act.wait_ge(o_turned.handle, o_turned.at(b))
            act.wait_ge(a_product.handle, a_product.at(b - 1))
            act.activation(oT[0][:], ps_s[:], ACT.Copy).then_inc(oT_hi.handle, 1)
            act.wait_ge(x2_turned.handle, x2_turned.at(b))
            act.wait_ge(x2T_out.handle, x2T_out.at(b - 1))
            act.wait_ge(r_product.handle, r_product.at(b - 1))
            act.wait_ge(ex[0]["x2_lo"].handle, ex[0]["x2_lo"].at(b - 1))
            act.activation(x2T[:], ps_s[:], ACT.Copy).then_inc(x2T_ready.handle, 1)
            act.wait_ge(r_step.handle, r_step.at(b))
            act.activation(lt[:], lg[:], ACT.Exp).then_inc(r_exp.handle, 1)

        def expert(e, b):
            s = ex[e]
            for f in range(FC):
                act.wait_ge(s["h_product"].handle, s["h_product"].at(b, f + 1))
                n = s["g_lo"].at(b, f - 3) if f >= 4 else s["g_lo"].at(b - 1)
                act.wait_ge(s["g_lo"].handle, n)
                act.wait_ge(s["g_hi"].handle, s["g_hi"].at(b, f - 3) if f >= 4 else s["g_hi"].at(b - 1))
                act.activation(g[:, f % 4, :], ps_l[:, f % 2, :], ACT.Gelu_apprx_tanh,
                               bias=bias[:, e, f:f + 1]).then_inc(s["gelu"].handle, 1)
            act.wait_ge(s["y_step"].handle, s["y_step"].at(b))
            act.wait_ge(s["y_turned"].handle, s["y_turned"].at(b - 1))
            for m in range(DC):
                act.activation(yT[:, m, :], ps_y[:, m, :], ACT.Identity,
                               bias=bias[:, e, FC + m:FC + m + 1]).then_inc(s["y_biased"].handle, 1)

        with act.Fori(0, B) as b:
            attention(b)
            expert(0, b)
        act.wait_ge(pb_ready, 2)
        act.wait_ge(ex[0]["g_lo"].handle, ex[0]["g_lo"].at(B - 1))
        act.wait_ge(ex[0]["g_hi"].handle, ex[0]["g_hi"].at(B - 1))
        act.wait_ge(ex[0]["y_turned"].handle, ex[0]["y_turned"].at(B - 1))
        with act.Fori(0, B) as b:
            expert(1, b)

    @block.gpsimd
    def _(pool):
        pool.memset(ident[:], 0.0).then_inc(consts_ready, 1)
        pool.wait_ge(consts_ready, 1)
        pool.affine_select(out=ident[:], in_=ident[:], compare_op=ALU.not_equal, fill=1.0, base=0,
                           pattern=[[-1, P]], channel_multiplier=1).then_inc(eye_ready, 1)
        pool.memset(ones[:], 1.0).then_inc(consts_ready, 1)
        pool.memset(ones_bf[:], 1.0).then_inc(consts_ready, 1)
        pool.memset(mhalf[:], -0.5).then_inc(consts_ready, 1)
        pool.memset(vbd[:], 0.0).then_inc(eye_ready, 1)
        pool.wait_ge(eye_ready, 2)
        root = float(DK) ** 0.5
        pool.memset(vbd[0:CT, :, 2 * DK:2 * DK + 1], root).then_inc(eye_ready, 1)
        pool.wait_ge(eye_ready, 3)
        pool.memset(vbd[CT:P, :, 2 * DK + 1:2 * DK + 2], root).then_inc(eye_ready, 1)
        pool.wait_ge(eye_ready, 4)
        for n in range(2):
            pool.memset(kbd[n][:].bitcast(F32), 0.0).then_inc(eye_ready, 1)

        def rsqrt(n, b):
            pool.wait_ge(ln[n]["var"].handle, ln[n]["var"].at(b))
            pool.tensor_tensor(rstd[:], var[:], mhalf[:], ALU.pow).then_inc(ln[n]["rstd"].handle, 1)

        def low_parts(e, b):
            s = ex[e]
            for f in range(FC):
                pool.wait_ge(s["g_hi"].handle, s["g_hi"].at(b, f + 1))
                pool.wait_ge(s["y_step"].handle, s["y_step"].at(b, f - 3) if f >= 4 else s["y_step"].at(b - 1))
                pool.tensor_tensor(gs[1][:, f % 4, :], g[:, f % 4, :], gs[0][:, f % 4, :].bitcast(F32), ALU.subtract).then_inc(s["g_lo"].handle, 1)

        with pool.Fori(0, B) as b:
            rsqrt(0, b)
            pool.wait_ge(xr_in.handle, xr_in.at(b))
            for t in range(NT):
                i = pool.tensor_tensor(xr[:, t, :], xr[:, t, :], bpb, ALU.add)
            i.then_inc(xr_biased.handle, 1)
            rsqrt(1, b)
            rsqrt(2, b)
            low_parts(0, b)
        pool.wait_ge(ex[0]["y_step"].handle, ex[0]["y_step"].at(B - 1))
        with pool.Fori(0, B) as b:
            low_parts(1, b)

    @block.vector
    def _(dve):
        def split(dst, src, hi_sem, lo_sem):
            dve.tensor_copy(dst[0], src).then_inc(*hi_sem[:2])
            dve.wait_ge(hi_sem[0], hi_sem[2])
            dve.tensor_tensor(dst[1], src, dst[0].bitcast(F32), ALU.subtract).then_inc(*lo_sem)

        dve.wait_ge(ld_small, 16 * 12)
        split([w[:].rearrange("p n c d -> p (n c d)") for w in wqkvp], stage,
              (proj_hi, 1, 1), (proj_lo, 1))
        for c in range(DC):
            dve.tensor_scalar(gw[:, c, :], wr[:, c, :], gam[:, c:c + 1], None, ALU.mult).then_inc(route_w, 1)
            dve.tensor_scalar(bw[:, c, :], wr[:, c, :], bet[:, c:c + 1], None, ALU.mult).then_inc(route_w, 1)
        dve.wait_ge(ctx_hi, 1)
        dve.tensor_tensor(cT[1][:], ps_m[:], cT[0][:].bitcast(F32), ALU.subtract).then_inc(ctx_lo, 1)
        for n, (src, row) in enumerate(((ps_s, bkb), (ps_y, bvb))):
            dve.wait_ge(kv_product, (n + 1) * KC)
            for k in range(KC):
                dve.tensor_tensor(kv[:, n, k, :], src[:, k // 2, (k % 2) * D:(k % 2) * D + D], row, ALU.add).then_inc(kv_biased, 1)
        dve.wait_ge(ld_w, 64)
        for n, (w, ws) in enumerate(((wraw[:, 0, :], w1s), (wraw[:, 1, :], w2s))):
            split([t[:] for t in ws], w, (w_hi, 1, n + 1), (w_lo, 1))
        dve.wait_ge(route_sum, 1)
        dve.tensor_copy(rc[:, 0, :], ps_m[:, 0, 0:E])
        dve.tensor_tensor(rc[:, 1, :], ps_m[:, 0, E:2 * E], brb[:], ALU.add).then_inc(route_ready, 1)
        dve.wait_ge(k_hi, 1)
        dve.tensor_tensor(kT[1][:], ps_l[:], kT[0][:].bitcast(F32), ALU.subtract).then_inc(k_lo, 1)

        def halfword(ap, upper):
            return ap.bitcast(U16).rearrange("p (n two) -> p n two", two=2)[:, :, upper]

        small = [(slice(0, FC), slice(0, FC)), (slice(FC, 2 * FC), slice(0, FC)),
                 (slice(2 * FC, 2 * FC + DC), slice(FC, FC + DC)), (slice(2 * FC + DC, 2 * (FC + DC)), slice(FC, FC + DC))]
        big_keys = [key[:, s, :] for s in range(4)]
        big_raw = [wraw[:, s // 2, :] for s in range(4)]
        small_keys = [skey[:, k] for k, _ in small]
        small_raw = [bias[:, 0, v] for _, v in small]
        for k, w in zip(big_keys + small_keys, big_raw + small_raw):
            dve.tensor_scalar(k, halfword(w, 1), 0x7FFF, None, ALU.bitwise_and).then_inc(key_ready, 1)
        for s, r in enumerate(RANKS):
            dve.memset(ranks[:, s:s + 1], float(r)).then_inc(state_ready, 1)
        dve.memset(prefix[:], 0.0).then_inc(state_ready, 1)
        dve.memset(below[:], 0.0).then_inc(state_ready, 1)
        dve.memset(half[:], float(2 ** (BITS - 1))).then_inc(state_ready, 1)
        dve.memset(cand[:], float(2 ** (BITS - 1) - 1)).then_inc(state_ready, 1)
        dve.wait_ge(state_ready, NS + 4)
        dve.wait_ge(key_ready, NS)

        def search_step(i):
            dve.wait_ge(cand_step.handle, cand_step.at(i - 1))
            for s in range(4):
                dve.wait_ge(ind_counted.handle, ind_counted.at(i, s - 1) if s >= 2 else ind_counted.at(i - 1))
                dve.tensor_scalar(ind[s % 2][:], big_keys[s], cand[:, s:s + 1], None, ALU.is_le).then_inc(ind_ready.handle, 1)
            dve.wait_ge(total_ready.handle, total_ready.at(i - 1))
            for s, (k, _) in enumerate(small):
                dve.tensor_scalar(sind[:, k], skey[:, k], cand[:, 4 + s:5 + s], None, ALU.is_le, ALU.add,
                                  accum_out=cnt[:, 4 + s:5 + s]).then_inc(cnt_ready.handle, 1)
            dve.wait_ge(ind_counted.handle, ind_counted.at(i))
            dve.tensor_copy(cnt[:, 0:4], ps_s[:, 0, 0:4]).then_inc(cnt_ready.handle, 1)
            dve.wait_ge(total_ready.handle, total_ready.at(i))
            dve.tensor_tensor(fail[:], ps_s[:, 1, 0:NS], ranks[:], ALU.is_lt).then_inc(failed.handle, 1)
            dve.wait_ge(failed.handle, failed.at(i))
            dve.tensor_tensor(fcnt[:], ps_s[:, 1, 0:NS], fail[:], ALU.mult).then_inc(below_step.handle, 1)
            dve.scalar_tensor_tensor(prefix[:], fail[:], half[:, 0:1], prefix[:], ALU.mult, ALU.add).then_inc(prefix_step.handle, 1)
            dve.wait_ge(prefix_step.handle, prefix_step.at(i, 1))
            dve.wait_ge(below_step.handle, below_step.at(i))
            dve.tensor_scalar(half[:], half[:], 0.5, None, ALU.mult).then_inc(prefix_step.handle, 1)
            dve.tensor_tensor(below[:], below[:], fcnt[:], ALU.max)
            dve.wait_ge(prefix_step.handle, prefix_step.at(i))
            dve.tensor_scalar(cand[:], prefix[:], half[:, 0:1], 1.0, ALU.add, ALU.subtract).then_inc(cand_step.handle, 1)

        with dve.Fori(0, BITS) as i:
            search_step(i)
        dve.wait_ge(cand_step.handle, cand_step.at(BITS - 1))
        dve.wait_ge(ind_counted.handle, ind_counted.at(BITS - 1))
        marks = [ind[s % 2][:].bitcast(U16) for s in range(4)] + [sind[:, k].bitcast(U16) for k, _ in small]
        for s, (k, w, mark) in enumerate(zip(big_keys + small_keys, big_raw + small_raw, marks)):
            dve.tensor_scalar(mark, k, prefix[:, s:s + 1], 65535.0, ALU.not_equal, ALU.mult).then_inc(key_mark, 1)
            dve.wait_ge(key_mark, s + 1)
            dve.tensor_tensor(k, mark, halfword(w, 0), ALU.max).then_inc(key_ready, 1)
        dve.tensor_copy(thr[:, :, 1], prefix[:]).then_inc(thr_ready, 1)
        dve.tensor_tensor(ranks[:], ranks[:], below[:], ALU.subtract).then_inc(state_ready, 1)
        dve.wait_ge(thr_ready, 1)
        dve.wait_ge(state_ready, NS + 5)
        dve.memset(prefix[:], 0.0).then_inc(state_ready, 1)
        dve.memset(below[:], 0.0).then_inc(state_ready, 1)
        dve.memset(half[:], float(2 ** (BITS - 1))).then_inc(state_ready, 1)
        dve.memset(cand[:], float(2 ** (BITS - 1) - 1)).then_inc(state_ready, 1)
        dve.wait_ge(state_ready, NS + 9)
        dve.wait_ge(key_ready, 2 * NS)
        with dve.Fori(BITS, 2 * BITS) as i:
            search_step(i)
        dve.wait_ge(cand_step.handle, cand_step.at(2 * BITS - 1))
        dve.tensor_copy(thr[:, :, 0], prefix[:]).then_inc(thr_ready, 1)
        dve.wait_ge(thr_ready, 2)
        limit = thr[:].rearrange("p s two -> p (s two)").bitcast(F32)

        steps = [0]

        def perturb(dst, w, mag, tr, s, done):
            def after(ins):
                steps[0] += 1
                ins.then_inc(tier_step, 1)
                dve.wait_ge(tier_step, steps[0])
            after(dve.tensor_scalar(mag.bitcast(U32), w.bitcast(U32), 0x7FFFFFFF, None, ALU.bitwise_and))
            after(dve.tensor_scalar(tr, mag, limit[:, s:s + 1], -2.0, ALU.is_ge, ALU.mult))
            after(dve.scalar_tensor_tensor(tr, mag, limit[:, s + 1:s + 2], tr, ALU.is_le, ALU.add))
            after(dve.tensor_scalar(tr, tr, -1.0, SCALE, ALU.max, ALU.mult))
            after(dve.tensor_tensor(tr, tr, w, ALU.mult))
            dve.tensor_tensor(dst, tr, w, ALU.add).then_inc(done, 1)

        def layer_norm(n, b, src, normalise=True):
            s = ln[n]
            for t in range(NT):
                dve.bn_stats(stat[:, t, :], src[:, t, :]).then_inc(s["stats"].handle, 1)
            dve.wait_ge(s["stats"].handle, s["stats"].at(b))
            dve.memset(carry[:], 0.0)
            for t in range(NT):
                dve.bn_aggr(mv[:, t, :], stat[:, t, :]).then_inc(s["mean"].handle, 1)
            dve.wait_ge(s["mean"].handle, s["mean"].at(b))
            dve.tensor_scalar(var[:], mv[:, :, 1], EPS, None, ALU.add).then_inc(s["var"].handle, 1)
            dve.wait_ge(s["rstd"].handle, s["rstd"].at(b))
            if normalise:
                for t in range(NT):
                    dve.tensor_scalar(xh[:, t, :], src[:, t, :], mv[:, t, 0:1], rstd[:, t:t + 1],
                                      ALU.subtract, ALU.mult).then_inc(s["xhat"].handle, 1)

        def attention(b):
            dve.wait_ge(x_in.handle, x_in.at(b))
            layer_norm(0, b, xa)
            dve.wait_ge(xT_hi.handle, xT_hi.at(b))
            dve.tensor_tensor(xhT[1][:], ps_m[:], xhT[0][:].bitcast(F32), ALU.subtract).then_inc(xT_lo.handle, 1)
            dve.wait_ge(q_in.handle, q_in.at(b))
            dve.wait_ge(s_product.handle, s_product.at(b - 1))
            split([t[:] for t in qs], qr[:], (q_hi.handle, 1, q_hi.at(b)), (q_lo.handle, 1))
            dve.wait_ge(mask_in.handle, mask_in.at(b))

            def masked(j):
                return sc[:, j % 2, :].rearrange("p (h k) -> p h k", k=CT)

            def shift(j):
                dve.wait_ge(s_product.handle, s_product.at(b, j + 1))
                dve.wait_ge(p_exp.handle, p_exp.at(b, j - 1) if j >= 2 else p_exp.at(b - 1))
                dve.tensor_tensor(masked(j), ps_s[:].rearrange("p a (h k) -> p (a h) k", k=CT),
                                  mk[:, j, :].unsqueeze(1).to_broadcast([P, H, CT]), ALU.mult).then_inc(s_masked.handle, 1)
                dve.wait_ge(s_masked.handle, s_masked.at(b, j + 1))
                dve.tensor_reduce(mx[:, j % 2, :], masked(j), AX.X, ALU.max).then_inc(s_max.handle, 1)
                dve.wait_ge(s_max.handle, s_max.at(b, j + 1))
                dve.tensor_tensor(masked(j), masked(j), mx[:, j % 2, :].unsqueeze(2).to_broadcast([P, H, CT]),
                                  ALU.subtract).then_inc(s_shifted.handle, 1)

            def normalise(j):
                o = ps_m[:, j % 2, 0:G * VW].rearrange("p (g v) -> p g v", v=VW)
                dve.wait_ge(o_product.handle, o_product.at(b, j + 1))
                dve.reciprocal(rs[:, j % 2, :].rearrange("p (g o) -> p g o", o=2), o[:, :, 2 * DK:VW]).then_inc(o_recip.handle, 1)
                dve.wait_ge(o_recip.handle, o_recip.at(b, j + 1))
                if j == 0:
                    dve.wait_ge(o_turned.handle, o_turned.at(b - 1))
                for a in range(2):
                    i = dve.tensor_tensor(
                        on[:, j, :].rearrange("p (g v) -> p g v", v=2 * DK)[:, :, a * DK:(a + 1) * DK],
                        o[:, :, a * DK:(a + 1) * DK],
                        rs[:, j % 2, :].rearrange("p (g o) -> p g o", o=2)[:, :, a:a + 1].to_broadcast([P, G, DK]), ALU.mult)
                i.then_inc(o_norm.handle, 1)

            shift(0)
            for j in range(NT):
                if j + 1 < NT:
                    shift(j + 1)
                if j >= 1:
                    normalise(j - 1)
            normalise(NT - 1)
            dve.wait_ge(oT_hi.handle, oT_hi.at(b))
            dve.tensor_tensor(oT[1][:], ps_s[:], oT[0][:].bitcast(F32), ALU.subtract).then_inc(oT_lo.handle, 1)
            dve.wait_ge(xr_biased.handle, xr_biased.at(b))
            for n in range(2):
                dve.wait_ge(a_product.handle, a_product.at(b, n + 1))
                dve.tensor_tensor(x2[:, 2 * n:2 * n + 2, :].rearrange("p t d -> p (t d)"), ps_m[:, n, :],
                                  xr[:, 2 * n:2 * n + 2, :].rearrange("p t d -> p (t d)"), ALU.add).then_inc(x2_ready.handle, 1)
            dve.wait_ge(x2_ready.handle, x2_ready.at(b))
            layer_norm(1, b, x2)
            dve.wait_ge(ln[1]["xhat"].handle, ln[1]["xhat"].at(b))
            layer_norm(2, b, xh, normalise=False)
            def step(n, ins):
                ins.then_inc(r_step.handle, 1)
                dve.wait_ge(r_step.handle, r_step.at(b, n))
            over = lambda ap: ap.unsqueeze(2).to_broadcast([P, NT, E])
            each = lambda ap: ap.unsqueeze(1).to_broadcast([P, NT, E])
            dve.wait_ge(r_product.handle, r_product.at(b))
            step(1, dve.tensor_tensor(lg[:], ps_m[:, 0, 0:NT * E].rearrange("p (t e) -> p t e", e=E), over(rstd[:]), ALU.mult))
            step(2, dve.tensor_tensor(nm[:], mv[:, :, 0], rstd[:], ALU.mult))
            step(3, dve.tensor_tensor(lt[:], each(rc[:, 0, :]), over(nm[:]), ALU.mult))
            step(4, dve.tensor_tensor(lg[:], lg[:], lt[:], ALU.subtract))
            step(5, dve.tensor_tensor(lg[:], lg[:], each(rc[:, 1, :]), ALU.add))
            step(6, dve.tensor_reduce(lmx[:], lg[:], AX.X, ALU.max))
            step(7, dve.tensor_tensor(lg[:], lg[:], over(lmx[:]), ALU.subtract))
            dve.wait_ge(r_exp.handle, r_exp.at(b))
            dve.tensor_reduce(s8[:], lt[:], AX.X, ALU.add).then_inc(r_sum.handle, 1)
            dve.tensor_reduce(s7[:], lt[:, :, 1:E], AX.X, ALU.add).then_inc(r_sum.handle, 1)
            dve.wait_ge(r_sum.handle, r_sum.at(b, 2))
            dve.reciprocal(s8[:], s8[:]).then_inc(r_sum.handle, 1)
            dve.wait_ge(r_sum.handle, r_sum.at(b))
            dve.wait_ge(ex[0]["acc_io"].handle, ex[0]["acc_io"].at(b - 1))
            dve.tensor_tensor(p0[:], lt[:, :, 0], s8[:], ALU.mult).then_inc(r_probs.handle, 1)
            dve.tensor_tensor(acc[:, :, D], s7[:], s8[:], ALU.mult).then_inc(r_probs.handle, 1)

        def expert(e, b):
            s = ex[e]
            if e == 1:
                dve.wait_ge(xt_in.handle, xt_in.at(b))
            dve.wait_ge(s["h_product"].handle, s["h_product"].at(b - 1))
            split([t[:] for t in x2s], x2T[:], (s["x2_hi"].handle, 1, s["x2_hi"].at(b)), (s["x2_lo"].handle, 1))
            for f in range(FC):
                dve.wait_ge(s["gelu"].handle, s["gelu"].at(b, f + 1))
                dve.wait_ge(s["y_step"].handle, s["y_step"].at(b, f - 3) if f >= 4 else s["y_step"].at(b - 1))
                dve.tensor_copy(gs[0][:, f % 4, :], g[:, f % 4, :]).then_inc(s["g_hi"].handle, 1)
            dve.wait_ge(s["y_turned"].handle, s["y_turned"].at(b))
            if e == 0:
                dve.wait_ge(r_probs.handle, r_probs.at(b))
            else:
                dve.wait_ge(s["acc_io"].handle, s["acc_io"].at(b))
            for t in range(NT):
                weight = p0[:, t:t + 1] if e == 0 else acc[:, t, D:D + 1]
                base = x2[:, t, :] if e == 0 else acc[:, t, 0:D]
                dve.scalar_tensor_tensor(acc[:, t, 0:D], ps_m[:, t // 2, (t % 2) * D:(t % 2) * D + D], weight, base,
                                         ALU.mult, ALU.add).then_inc(s["mixed"].handle, 1)

        with dve.Fori(0, B) as b:
            attention(b)
            expert(0, b)
        dve.wait_ge(ld_again, 32)
        mag = key[:, 0:2].rearrange("p a n -> p (a n)").bitcast(F32)
        for n, ws in enumerate((w1s, w2s)):
            w = wagain[:, n, :]
            perturb(w, w, mag, tier, 2 * n, pw_ready)
            dve.wait_ge(pw_ready, n + 1)
            last = ex[0]["h_product"] if n == 0 else ex[0]["y_step"]
            dve.wait_ge(last.handle, last.at(B - 1))
            split([t[:] for t in ws], w, (pw_hi, 1, n + 1), (pw_lo, 1))
        for part, s in ((slice(0, FC), 4), (slice(FC, FC + DC), 6)):
            perturb(bias[:, 1, part], bias[:, 0, part], sabs[:, part], tier[:, part], s, pb_ready)
        with dve.Fori(0, B) as b:
            expert(1, b)

    ctx.close()


_INS = ["x", "ctx_1024", "mask_BxSxS2_ff1", "L0_xattn_WQ", "L0_xattn_bQ", "L0_xattn_WK", "L0_xattn_bK",
        "L0_xattn_WV", "L0_xattn_bV", "L0_xattn_Wp", "L0_xattn_bp", "L0_ffn_W1", "L0_ffn_b1", "L0_ffn_W2",
        "L0_ffn_b2", "L0_ffn_ln_gamma", "L0_ffn_ln_beta", "L0_ffn_Wr", "L0_ffn_br"]


def kernel(**inputs):
    import numpy as np
    import concourse.bacc as bacc
    from concourse.bass_utils import run_bass_kernel_spmd

    nc = bacc.Bacc("TRN2", target_bir_lowering=False, num_devices=1)
    arrays, args = {}, []
    for name in _INS:
        a = np.ascontiguousarray(inputs[name])
        arrays["in_" + name] = a
        args.append(nc.dram_tensor("in_" + name, a.shape, mybir.dt.from_np(a.dtype), kind="ExternalInput").ap())
    args.append(nc.dram_tensor("out_x", inputs["x"].shape, F32, kind="ExternalOutput").ap())
    build_program(nc, *args)
    return run_bass_kernel_spmd(nc, [arrays], core_ids=[0]).results[0]["out_x"]
```

```python
from contextlib import ExitStack

import concourse.bass as bass
from concourse import mybir

ALU = mybir.AluOpType
ACT = mybir.ActivationFunctionType
AX = mybir.AxisListType
F32 = mybir.dt.float32
F32R = mybir.dt.float32r
BF16 = mybir.dt.bfloat16
U16 = mybir.dt.uint16
U32 = mybir.dt.uint32

P = 128
EPS = 1e-5
SPARSITY = 0.1
SCALE = 0.8
BITS = 16


class Signal:

    def __init__(self, handle, per):
        self.handle, self.per = handle, per

    def at(self, batch, count=None):
        return (batch + 1) * self.per + (self.per if count is None else count)


def build_program(nc, x, ctx_in, mask, WQ, bQ, WK, bK, WV, bV, Wp, bp,
                  W1, b1, W2, b2, gamma, beta, Wr, br, out):
    B, S, D = x.shape
    CT = ctx_in.shape[1]
    F = W1.shape[1]
    E = Wr.shape[1]
    H = 16
    DK = D // H
    NT = S // P
    DC = D // P
    FC = F // P
    HH = H // 2
    R = S // H
    C = S // R
    G = H // 2
    VW = 2 * DK + 2
    KC = B * CT // P
    assert (P, DC, R * C, HH * DK, 2 * CT, HH * CT) == (128, 2, S, P, P, 512)

    def rank(n, top):
        k = max(1, int(n * SPARSITY / 2))
        return n - k + 1 if top else k
    SEARCH_N = [D * F, D * F, D * F, D * F, F, F, D, D]
    RANKS = [rank(n, s % 2 == 0) for s, n in enumerate(SEARCH_N)]
    NS = len(RANKS)
    WN = D * F // P

    ctx = ExitStack()

    def sb(name, shape, dt=F32):
        return ctx.enter_context(nc.sbuf_tensor(name, shape, dt))

    def sig(name, per=1):
        s = Signal(ctx.enter_context(nc.semaphore(name)), per)
        signals.append(s)
        return s

    def sem(name):
        return ctx.enter_context(nc.semaphore(name))

    signals = []

    ps_s, ps_l, ps_y, ps_m = (ctx.enter_context(nc.psum_tensor(f"ps_{n}", [P, 2, 512], F32)) for n in "slym")

    q_scr = nc.dram_tensor("q_scr", [B, D, S], F32, kind="Internal").ap()
    v_scr = nc.dram_tensor("v_scr", [B, CT, D], F32, kind="Internal").ap()
    k_scr = nc.dram_tensor("k_scr", [B, CT, D], F32, kind="Internal").ap()
    kh_scr = nc.dram_tensor("kh_scr", [2, P, DC * B * CT], F32, kind="Internal").ap()
    xt_scr = nc.dram_tensor("xt_scr", [B, P, DC * S], F32, kind="Internal").ap()
    acc_scr = nc.dram_tensor("acc_scr", [B, P, NT * (D + 1)], F32, kind="Internal").ap()

    def view(region, start, *shape):
        n = 1
        for d in shape:
            n *= d
        ap = region[:, start:start + n]
        if len(shape) == 1:
            return ap
        names = "abc"[:len(shape)]
        return ap.rearrange("p (" + " ".join(names) + ") -> p " + " ".join(names), **dict(zip(names[1:], shape[1:])))

    region_a = sb("region_a", [P, 6 * H * CT])
    region_b = sb("region_b", [P, 2 * WN])
    region_c = [sb(f"region_c_{n}", [P, 4 * S], F32R) for n in ("hi", "lo")]
    region_d = [sb(f"region_d_{n}", [P, DC * S], F32R) for n in ("hi", "lo")]
    stage = view(region_a, 0, 4 * DC * D)
    ctxt = view(region_a, 4 * DC * D, KC, D)
    kv = view(region_a, 4 * DC * D + KC * D, 2, KC, D)
    kk = view(region_a, 4 * DC * D + 3 * KC * D, KC, D)
    sc = view(region_a, 0, 2, H * CT)
    pr = view(region_a, 2 * H * CT, 2, H * CT)
    pT = view(region_a, 4 * H * CT, 2, G * P)
    wraw = view(region_b, 0, 2, WN)
    x2T = view(region_b, 0, DC, S)
    yT = view(region_b, DC * S, DC, S)
    g = view(region_b, 2 * DC * S, 4, S)
    wagain = view(region_a, 0, 2, WN)
    tier = view(region_a, 2 * WN, WN)
    cT = [view(r, 0, DC, B * CT) for r in region_c]
    kT = [view(r, DC * B * CT, DC, B * CT) for r in region_c]
    gs = [view(r, 0, 4, S) for r in region_c]
    wkv = [view(r, 0, 2, DC, D) for r in region_d]
    oT = [view(r, 0, DC, S) for r in region_d]

    ident = sb("ident", [P, P])
    ones = sb("ones", [P, P])
    ones_bf = sb("ones_bf", [P, 2], BF16)
    mhalf = sb("mhalf", [P, NT])
    wqp = [sb(f"wqp_{n}", [P, 2, DC, D], F32R) for n in ("hi", "lo")]
    bq = sb("bq", [P, DC])
    rows = sb("rows", [P, 3, D])
    bkb, bvb, bpb = (rows[:, n, :] for n in range(3))
    w1s = [sb(f"w1_{n}", [P, DC * F], F32R) for n in ("hi", "lo")]
    w2s = [sb(f"w2_{n}", [P, FC * D], F32R) for n in ("hi", "lo")]
    bias = sb("bias", [P, 2, FC + DC])
    gam = sb("gam", [P, DC])
    bet = sb("bet", [P, DC])
    wr = sb("wr", [P, DC, E])
    gw = sb("gw", [P, DC, E])
    bw = sb("bw", [P, DC, E])
    brb = sb("brb", [P, E])
    rc = sb("rc", [P, 2, E])

    key = sb("key", [P, 4, WN], U16)
    skey = sb("skey", [P, 2 * (FC + DC)], U16)
    ind = [sb(f"ind{n}", [P, WN], BF16) for n in range(2)]
    sind = sb("sind", [P, 2 * (FC + DC)], BF16)
    sabs = sb("sabs", [P, FC + DC])
    ranks = sb("ranks", [P, NS])
    prefix = sb("prefix", [P, NS])
    cand = sb("cand", [P, NS])
    half = sb("half", [P, 1])
    below = sb("below", [P, NS])
    cnt = sb("cnt", [P, NS])
    fail = sb("fail", [P, NS])
    fcnt = sb("fcnt", [P, NS])
    thr = sb("thr", [P, NS, 2], U16)

    xa = sb("xa", [P, NT, D])
    x2 = sb("x2", [P, NT, D])
    keep = sb("keep", [P, NT, D])
    mk = sb("mk", [P, NT, CT])
    stat = sb("stat", [P, NT, 6])
    mv = [sb(f"mv{n}", [P, NT, 2]) for n in range(3)]
    var = [sb(f"var{n}", [P, NT]) for n in range(3)]
    rstd = [sb(f"rstd{n}", [P, NT]) for n in range(3)]
    nmean = [sb(f"nmean{n}", [P, NT]) for n in range(3)]
    shiftby = [sb(f"shiftby{n}", [P, NT]) for n in range(3)]
    carry = sb("carry", [P, 1])
    tick = sb("tick", [P, 1])
    xh = [sb(f"xh{n}", [P, NT, D]) for n in range(2)]
    xhT = [sb(f"xhT_{n}", [P, DC, S], F32R) for n in ("hi", "lo")]
    qf = sb("qf", [P, DC, S])
    qr = sb("qr", [P, DC, S])
    qs = [sb(f"qs_{n}", [P, DC, S], F32R) for n in ("hi", "lo")]
    kbd = [sb(f"kbd_{n}", [P, DC, HH, CT], F32R) for n in ("hi", "lo")]
    vbd = sb("vbd", [P, G, VW])
    mx = sb("mx", [P, 2, H])
    rs = sb("rs", [P, 2, H])
    on = sb("on", [P, NT, D])

    x2s = [sb(f"x2s_{n}", [P, DC, S], F32R) for n in ("hi", "lo")]
    lg = sb("lg", [P, NT, E])
    lt = sb("lt", [P, NT, E])
    lmx = sb("lmx", [P, NT])
    s8 = sb("s8", [P, NT])
    s7 = sb("s7", [P, NT])
    p0 = sb("p0", [P, NT])
    acc = sb("acc", [P, NT, D + 1])

    ld_w4 = sem("ld_w4")
    ld_small = sem("ld_small")
    ld_ctx = sem("ld_ctx")
    ld_w = sem("ld_w")
    ld_again = sem("ld_again")
    consts_ready = sem("consts_ready")
    eye_ready = sem("eye_ready")
    proj_hi = sem("proj_hi")
    proj_lo = sem("proj_lo")
    ctx_turned = sem("ctx_turned")
    ctx_hi = sem("ctx_hi")
    ctx_lo = sem("ctx_lo")
    kv_product = sem("kv_product")
    kv_biased = sem("kv_biased")
    kv_out = sem("kv_out")
    kk_in = sem("kk_in")
    k_turned = sem("k_turned")
    k_hi = sem("k_hi")
    k_lo = sem("k_lo")
    kh_out = sem("kh_out")
    w_hi = sem("w_hi")
    w_lo = sem("w_lo")
    route_w = sem("route_w")
    route_sum = sem("route_sum")
    route_ready = sem("route_ready")
    key_ready = sem("key_ready")
    state_ready = sem("state_ready")
    key_mark = sem("key_mark")
    thr_ready = sem("thr_ready")
    tier_step = sem("tier_step")
    pw_ready = sem("pw_ready")
    pw_hi = sem("pw_hi")
    pw_lo = sem("pw_lo")
    pb_ready = sem("pb_ready")

    ind_ready = sig("ind_ready", 4)
    ind_counted = sig("ind_counted", 4)
    cnt_ready = sig("cnt_ready", 5)
    total_ready = sig("total_ready")
    failed = sig("failed")
    below_step = sig("below_step")
    prefix_step = sig("prefix_step", 2)
    cand_step = sig("cand_step")

    x_in = sig("x_in", 16)
    xr_in = sig("xr_in", 16 * NT)
    keep_in = sig("keep_in", 16)
    mask_in = sig("mask_in", 16 * NT)
    v_in = sig("v_in", 32)
    k_in = sig("k_in", 16 * 2 * HH)
    q_out = sig("q_out", 16)
    q_in = sig("q_in", 16 * H)
    ln = [dict(stats=sig(f"ln{n}_stats", NT), mean=sig(f"ln{n}_mean", NT), var=sig(f"ln{n}_var", 2),
               rstd=sig(f"ln{n}_rstd"), shift=sig(f"ln{n}_shift"), xhat=sig(f"ln{n}_xhat", NT)) for n in range(3)]
    xT_turned = sig("xT_turned")
    xT_hi = sig("xT_hi")
    xT_lo = sig("xT_lo")
    q_product = sig("q_product", DC)
    q_biased = sig("q_biased", DC)
    q_hi = sig("q_hi")
    q_lo = sig("q_lo")
    s_product = sig("s_product", NT)
    s_masked = sig("s_masked", NT)
    s_max = sig("s_max", NT)
    s_shifted = sig("s_shifted", NT)
    p_exp = sig("p_exp", NT)
    p_turned = sig("p_turned", NT)
    pT_ready = sig("pT_ready", NT)
    o_product = sig("o_product", NT)
    o_recip = sig("o_recip", NT)
    o_norm = sig("o_norm", NT)
    o_turned = sig("o_turned")
    oT_hi = sig("oT_hi")
    oT_lo = sig("oT_lo")
    a_product = sig("a_product", 2)
    xr_biased = sig("xr_biased")
    x2_ready = sig("x2_ready", 2)
    x2_turned = sig("x2_turned")
    x2T_ready = sig("x2T_ready")
    x2T_out = sig("x2T_out", 16)
    r_product = sig("r_product")
    r_step = sig("r_step", 6)
    r_exp = sig("r_exp")
    r_sum = sig("r_sum", 3)
    r_probs = sig("r_probs", 2)

    ex = [dict(
        x2_hi=sig(f"e{e}_x2_hi"), x2_lo=sig(f"e{e}_x2_lo"),
        h_product=sig(f"e{e}_h_product", FC), gelu=sig(f"e{e}_gelu", FC),
        g_hi=sig(f"e{e}_g_hi", FC), g_lo=sig(f"e{e}_g_lo", FC),
        y_step=sig(f"e{e}_y_step", FC), y_biased=sig(f"e{e}_y_biased", DC),
        y_turned=sig(f"e{e}_y_turned"), mixed=sig(f"e{e}_mixed", NT),
        acc_io=sig(f"e{e}_acc_io", 16), out_io=sig(f"e{e}_out_io", 16 * NT)) for e in range(2)]
    xt_in = sig("xt_in", 16)

    def perm(ap):
        return ap.rearrange("(r c) d -> c r d", c=C)

    def three(eng, out_ap, a, b, first=True, last=True):
        eng.matmul(out_ap, a[0], b[0], start=first, stop=False)
        eng.matmul(out_ap, a[0], b[1], start=False, stop=False)
        return eng.matmul(out_ap, a[1], b[0], start=False, stop=last)

    def wait(eng, signal, batch, count=None):
        value = signal.at(batch, count)
        if not (isinstance(value, int) and value <= 0):
            eng.wait_ge(signal.handle, value)

    with nc.Block() as credit:
        @credit.gpsimd
        def _(pool):
            for s in signals:
                pool.sem_inc(s.handle, s.per)

    def pipeline(eng, body, between, last_expert):
        body(0, 0, first=True)
        with eng.Fori(1, B // 2) as i:
            body(i, 0)
        between()
        with eng.Fori(B // 2, B - 1) as i:
            body(i, 1)
        body(B - 1, 1, last=True)
        last_expert()

    block = ctx.enter_context(nc.Block())

    @block.sync
    def _(sp):
        def load_x(b):
            wait(sp, ln[0]["xhat"], b - 1)
            sp.dma_start(xa[:], x[b].rearrange("(t p) d -> p t d", p=P)).then_inc(x_in.handle, 16)

        def load_residual(b):
            wait(sp, ln[1]["xhat"], b - 1)
            wait(sp, keep_in, b - 1)
            for j in range(NT):
                sp.dma_start(x2[:, j, :], perm(x[b])[4 * j:4 * j + 4]).then_inc(xr_in.handle, 16)

        def queries(b):
            wait(sp, q_biased, b)
            sp.dma_start(q_scr[b].rearrange("(m p) s -> p m s", p=P), qf[:]).then_inc(q_out.handle, 16)
            wait(sp, q_out, b)
            wait(sp, q_lo, b - 1)
            for h in range(H):
                sp.dma_start(qr[DK * (h % HH):DK * (h % HH) + DK, h // HH].rearrange("p (c r) -> p c r", r=R),
                             q_scr[b].rearrange("(c d) (h r) -> h d c r", d=DK, r=R)[h]).then_inc(q_in.handle, 16)

        def load_context(b):
            wait(sp, s_masked, b - 1)
            for j in range(NT):
                sp.dma_start(mk[:, j, :], perm(mask[b])[4 * j:4 * j + 4]).then_inc(mask_in.handle, 16)
            wait(sp, s_product, b - 1)
            for h in range(HH):
                for n in range(2):
                    sp.dma_start(kbd[n][DK * h:DK * h + DK, :, h, :].bitcast(F32),
                                 kh_scr[n, DK * h:DK * h + DK].rearrange("p (c b k) -> b p c k", k=CT, c=DC)[b]).then_inc(k_in.handle, 16)
            wait(sp, o_product, b - 1)
            for o in range(2):
                sp.dma_start(vbd[CT * o:CT * o + CT, :, DK * o:DK * o + DK],
                             v_scr[b].rearrange("t (c d) -> (t c) d", d=DK).rearrange("(g o k) d -> o k g d", k=CT, o=2)[o]).then_inc(v_in.handle, 16)

        with nc.allow_non_contiguous_dma(reason="small vectors laid out by partition"):
            for k in range(KC):
                sp.dma_start(ctxt[:, k, :], ctx_in.rearrange("b t d -> (b t) d")[k * P:(k + 1) * P]).then_inc(ld_ctx, 16)
            load_x(0)
            for n, w in enumerate((WQ, WK, WV, Wp)):
                sp.dma_start(view(region_a, n * DC * D, DC, D), w.rearrange("(c p) n -> p c n", p=P)).then_inc(ld_w4, 16)
            for n, v in enumerate((bK, bV, bp)):
                sp.dma_start(rows[:, n, :], v.rearrange("(a d) -> a d", a=1).to_broadcast([P, D])).then_inc(ld_small, 16)
            sp.dma_start(bq[:], bQ.rearrange("(c p) -> p c", p=P)).then_inc(ld_small, 16)
            sp.dma_start(wraw[:, 0].rearrange("p (c f) -> p c f", c=DC), W1.rearrange("(c p) f -> p c f", p=P)).then_inc(ld_w, 16)
            sp.dma_start(wraw[:, 1].rearrange("p (c d) -> p c d", c=FC), W2.rearrange("(c p) d -> p c d", p=P)).then_inc(ld_w, 16)
            sp.dma_start(bias[:, 0, 0:FC], b1.rearrange("(c p) -> p c", p=P)).then_inc(ld_w, 16)
            sp.dma_start(bias[:, 0, FC:FC + DC], b2.rearrange("(c p) -> p c", p=P)).then_inc(ld_w, 16)
            sp.dma_start(gam[:], gamma.rearrange("(c p) -> p c", p=P)).then_inc(ld_small, 16)
            sp.dma_start(bet[:], beta.rearrange("(c p) -> p c", p=P)).then_inc(ld_small, 16)
            sp.dma_start(wr[:], Wr.rearrange("(c p) e -> p c e", p=P)).then_inc(ld_small, 16)
            sp.dma_start(brb[:], br.rearrange("(a e) -> a e", a=1).to_broadcast([P, E])).then_inc(ld_small, 16)
        sp.wait_ge(kv_biased, 2 * KC)
        sp.dma_start(k_scr.rearrange("b t d -> (b t) d").rearrange("(k p) d -> p k d", p=P), kv[:, 0]).then_inc(kv_out, 16)
        sp.dma_start(v_scr.rearrange("b t d -> (b t) d").rearrange("(k p) d -> p k d", p=P), kv[:, 1]).then_inc(kv_out, 16)
        sp.wait_ge(kv_out, 32)
        for b in range(B):
            sp.dma_start(kk[CT * (b % 2):CT * (b % 2) + CT, b // 2].rearrange("k (h d) -> k h d", d=DK),
                         k_scr[b].rearrange("t (c d) -> (t c) d", d=DK).rearrange("(h k) d -> k h d", k=CT)).then_inc(kk_in, 16)
        queries(0)
        sp.wait_ge(k_lo, 1)
        for n in range(2):
            sp.dma_start(kh_scr[n], kT[n].rearrange("p c k -> p (c k)").bitcast(F32)).then_inc(kh_out, 16)
        sp.wait_ge(kh_out, 32)
        sp.wait_ge(eye_ready, 6)
        load_context(0)

        def put_expert(b):
            wait(sp, ex[0]["mixed"], b)
            sp.dma_start(acc_scr[b], acc[:].rearrange("p t d -> p (t d)")).then_inc(ex[0]["acc_io"].handle, 16)

        def body(i, rnd, first=False, last=False):
            if not last:
                load_x(i + 1)
            load_residual(i)
            if not last:
                queries(i + 1)
                load_context(i + 1)
            wait(sp, x2T_ready, i)
            sp.dma_start(xt_scr[i], x2T.rearrange("p c s -> p (c s)")).then_inc(x2T_out.handle, 16)
            if not first:
                put_expert(i - 1)
            wait(sp, x2_ready, i)
            wait(sp, ex[0]["mixed"], i - 1)
            sp.dma_start(keep[:], x2[:]).then_inc(keep_in.handle, 16)

        def last_expert():
            wait(sp, o_product, B - 1)
            sp.dma_start(wagain[:, 0].rearrange("p (c f) -> p c f", c=DC), W1.rearrange("(c p) f -> p c f", p=P)).then_inc(ld_again, 16)
            sp.dma_start(wagain[:, 1].rearrange("p (c d) -> p c d", c=FC), W2.rearrange("(c p) d -> p c d", p=P)).then_inc(ld_again, 16)
            put_expert(B - 1)

        pipeline(sp, body, lambda: None, last_expert)
        wait(sp, x2T_out, B - 1)
        wait(sp, ex[0]["acc_io"], B - 1)
        s = ex[1]

        def load_batch(b):
            wait(sp, s["x2_lo"], b - 1)
            sp.dma_start(x2T.rearrange("p c s -> p (c s)"), xt_scr[b]).then_inc(xt_in.handle, 16)

        def load_acc(b):
            wait(sp, s["out_io"], b - 1)
            sp.dma_start(acc[:].rearrange("p t d -> p (t d)"), acc_scr[b]).then_inc(s["acc_io"].handle, 16)

        def store(b):
            wait(sp, s["mixed"], b)
            for j in range(NT):
                sp.dma_start(perm(out[b])[4 * j:4 * j + 4], acc[:, j, 0:D]).then_inc(s["out_io"].handle, 16)

        load_batch(0)
        load_acc(0)
        with sp.Fori(1, B) as b:
            load_batch(b)
            store(b - 1)
            load_acc(b)
        store(B - 1)
        wait(sp, ex[1]["out_io"], B - 1)

    @block.tensor
    def _(pe):
        def w_of(n, c, cols):
            return [w[:, n, c, cols] for w in wqp]

        def turn_queries_input(b):
            wait(pe, ln[0]["xhat"], b)
            wait(pe, ex[0]["y_biased"], b - 3)
            for c in range(DC):
                for t in range(NT):
                    mm = pe.transpose(ps_y[:, c, t * P:(t + 1) * P], xh[0][:, t, c * P:(c + 1) * P], ident[:])
            mm.then_inc(xT_turned.handle, 1)

        def queries(b):
            wait(pe, xT_hi, b)
            wait(pe, xT_lo, b)
            for m in range(DC):
                for c in range(DC):
                    mm = three(pe, ps_y[:, m, :], w_of(0, c, slice(m * P, (m + 1) * P)),
                               [t[:, c, :] for t in xhT], c == 0, c == DC - 1)
                mm.then_inc(q_product.handle, 1)

        def scores(b, j):
            if j == 0:
                wait(pe, q_hi, b)
                wait(pe, q_lo, b)
                wait(pe, k_in, b)
                wait(pe, ex[0]["mixed"], b - 2)
            else:
                wait(pe, s_masked, b, j)
            for m in range(DC):
                mm = three(pe, ps_s[:, m, :], [t[:, m, j * P:(j + 1) * P] for t in qs],
                           [t[:, m].rearrange("p h k -> p (h k)") for t in kbd])
            mm.then_inc(s_product.handle, 1)

        def turn_probs(b, j):
            wait(pe, p_exp, b, j + 1)
            if j == 0:
                wait(pe, ex[0]["g_hi"], b - 2)
            else:
                wait(pe, pT_ready, b, j)
            for n in range(G):
                mm = pe.transpose(ps_l[:, n // 4, (n % 4) * P:(n % 4 + 1) * P], pr[:, j % 2, n * P:(n + 1) * P], ident[:])
            mm.then_inc(p_turned.handle, 1)

        def values(b, j):
            wait(pe, pT_ready, b, j + 1)
            if j == 0:
                wait(pe, v_in, b)
                wait(pe, r_step, b - 1, 1)
            else:
                wait(pe, o_norm, b, j)
            for n in range(G):
                mm = pe.matmul(ps_m[:, 0, n * VW:(n + 1) * VW], pT[:, j % 2, n * P:(n + 1) * P], vbd[:, n, :],
                               start=True, stop=True)
            mm.then_inc(o_product.handle, 1)

        def turn_output(b):
            wait(pe, o_norm, b)
            wait(pe, s_masked, b)
            for c in range(DC):
                for t in range(NT):
                    mm = pe.transpose(ps_s[:, c, t * P:(t + 1) * P], on[:, t, c * P:(c + 1) * P], ident[:])
            mm.then_inc(o_turned.handle, 1)

        def project(b):
            wait(pe, oT_hi, b)
            wait(pe, oT_lo, b)
            for t in range(NT):
                for c in range(DC):
                    mm = three(pe, ps_s[:, t // 2, (t % 2) * D:(t % 2) * D + D],
                               [o[:, c, t * P:(t + 1) * P] for o in oT], w_of(1, c, slice(0, D)), c == 0, c == DC - 1)
                if t % 2:
                    mm.then_inc(a_product.handle, 1)

        def turn_x2(b):
            wait(pe, ln[1]["xhat"], b)
            wait(pe, x2_ready, b)
            for c in range(DC):
                for t in range(NT):
                    mm = pe.transpose(ps_s[:, c, t * P:(t + 1) * P], xh[1][:, t, c * P:(c + 1) * P], ident[:])
            mm.then_inc(x2_turned.handle, 1)

        def router(b):
            wait(pe, x2T_ready, b)
            for t in range(NT):
                for c in range(DC):
                    mm = pe.matmul(ps_m[:, 0, t * E:(t + 1) * E], x2T[:, c, t * P:(t + 1) * P], gw[:, c, :],
                                   start=c == 0, stop=c == DC - 1)
            mm.then_inc(r_product.handle, 1)

        def hidden(e, b, f):
            s = ex[e]
            if f == 0:
                wait(pe, s["x2_hi"], b)
                wait(pe, s["x2_lo"], b)
                if e == 0:
                    wait(pe, pT_ready, b + 1 if not isinstance(b, int) or b + 1 < B else b)
            if f >= 2:
                wait(pe, s["g_hi"], b, f - 1)
            elif e == 1:
                wait(pe, s["g_hi"], b - 1)
            for c in range(DC):
                mm = three(pe, ps_l[:, f % 2, :], [w[:, c * F + f * P:c * F + (f + 1) * P] for w in w1s],
                           [t[:, c, :] for t in x2s], c == 0, c == DC - 1)
            mm.then_inc(s["h_product"].handle, 1)

        def output(e, b, f):
            s = ex[e]
            if f == 0:
                wait(pe, s["y_biased"], b - 1)
                if e == 0:
                    wait(pe, q_biased, b + 1 if not isinstance(b, int) or b + 1 < B else b)
                    if not isinstance(b, int) or b + 2 < B:
                        wait(pe, q_biased, b + 2)
            wait(pe, s["g_lo"], b, f + 1)
            for m in range(DC):
                mm = three(pe, ps_y[:, m, :], [w[:, f * D + m * P:f * D + (m + 1) * P] for w in w2s],
                           [t[:, f % 4, :] for t in gs], f == 0, f == FC - 1)
            mm.then_inc(s["y_step"].handle, 1)

        def turn_y(e, b, dst):
            s = ex[e]
            wait(pe, s["y_biased"], b)
            if e == 0:
                wait(pe, x2T_ready, b + 1 if not isinstance(b, int) or b + 1 < B else b)
            wait(pe, s["mixed"], b - 1)
            for t in range(NT):
                for c in range(DC):
                    mm = pe.transpose(dst[:, t // 2, (t % 2) * D + c * P:(t % 2) * D + (c + 1) * P],
                                      yT[:, c, t * P:(t + 1) * P], ident[:])
            mm.then_inc(s["y_turned"].handle, 1)

        def count(k, pair):
            for s in (2 * pair, 2 * pair + 1):
                wait(pe, ind_ready, k, s + 1)
                if s == 0:
                    wait(pe, below_step, k - 1)
                for c in range(WN // P):
                    mm = pe.matmul(ps_m[:, 1, s:s + 1], ind[s % 2][:, c * P:(c + 1) * P], ones_bf[:, 0:1],
                                   start=c == 0, stop=c == WN // P - 1)
                mm.then_inc(ind_counted.handle, 1)

        def total(k):
            wait(pe, cnt_ready, k)
            pe.matmul(ps_m[:, 1, NS:2 * NS], ones[:], cnt[:], start=True, stop=True).then_inc(total_ready.handle, 1)

        pe.wait_ge(ld_ctx, 16 * KC)
        pe.wait_ge(eye_ready, 1)
        for c in range(DC):
            for k in range(KC):
                mm = pe.transpose(ps_m[:, c, k * P:(k + 1) * P], ctxt[:, k, c * P:(c + 1) * P], ident[:])
        mm.then_inc(ctx_turned, 1)
        pe.wait_ge(proj_lo, 2)
        pe.wait_ge(ctx_lo, 1)
        for n, dst in ((0, ps_s), (1, ps_l)):
            for k in range(KC):
                for c in range(DC):
                    mm = three(pe, dst[:, k // 2, (k % 2) * D:(k % 2) * D + D],
                               [t[:, c, k * P:(k + 1) * P] for t in cT], [w[:, n, c, :] for w in wkv],
                               c == 0, c == DC - 1)
                mm.then_inc(kv_product, 1)
        turn_queries_input(0)
        queries(0)
        pe.wait_ge(kk_in, 16 * B)
        for c in range(DC):
            for k in range(KC):
                mm = pe.transpose(ps_m[:, c, k * P:(k + 1) * P], kk[:, k, c * P:(c + 1) * P], ident[:])
        mm.then_inc(k_turned, 1)
        pe.wait_ge(consts_ready, 4)
        pe.wait_ge(route_w, 2 * DC)
        pe.wait_ge(kv_biased, 2 * KC)
        for n, w in enumerate((gw, bw)):
            for c in range(DC):
                mm = pe.matmul(ps_s[:, 0, n * E:(n + 1) * E], ones[:], w[:, c, :], start=c == 0, stop=c == DC - 1)
        mm.then_inc(route_sum, 1)
        pe.wait_ge(route_ready, 1)
        pe.wait_ge(k_lo, 1)
        pe.wait_ge(w_lo, 2)

        def body(i, rnd, first=False, last=False):
            k = 4 * i
            scores(i, 0)
            count(k, 0)
            scores(i, 1)
            turn_probs(i, 0)
            scores(i, 2)
            count(k, 1)
            turn_probs(i, 1)
            values(i, 0)
            if not last:
                turn_queries_input(i + 1)
            scores(i, 3)
            total(k)
            turn_probs(i, 2)
            values(i, 1)
            count(k + 1, 0)
            turn_probs(i, 3)
            values(i, 2)
            if not last:
                queries(i + 1)
            values(i, 3)
            count(k + 1, 1)
            work = [
                lambda: total(k + 1),
                lambda: turn_output(i),
                lambda: count(k + 2, 0),
                lambda: project(i),
                lambda: count(k + 2, 1),
                lambda: total(k + 2),
                lambda: turn_x2(i),
                lambda: count(k + 3, 0),
                lambda: count(k + 3, 1),
                lambda: total(k + 3),
                lambda: router(i),
            ]
            places = {0: ["h0", "h1"], 1: ["h2"], 2: ["h3", "o0"], 3: ["o1", "h4"], 4: ["h5", "o2"],
                      5: ["o3", "h6"], 6: ["o4", "h7"], 7: ["o5"], 8: ["o6"], 9: ["o7"]}
            for n, do in enumerate(work):
                if not first:
                    for p in places.get(n, []):
                        (hidden if p[0] == "h" else output)(0, i - 1, int(p[1]))
                do()
            if not first:
                turn_y(0, i - 1, ps_s)

        def expert_alone(e, b, before_turn=None):
            for f in range(FC):
                hidden(e, b, f)
                if f == 1 and before_turn is not None:
                    before_turn()
                if f >= 3:
                    output(e, b, f - 3)
            for f in range(FC - 3, FC):
                output(e, b, f)

        def last_expert():
            expert_alone(0, B - 1)
            turn_y(0, B - 1, ps_s)

        pipeline(pe, body, lambda: None, last_expert)
        pe.wait_ge(pw_lo, 2)
        wait(pe, ex[0]["g_hi"], B - 1)
        expert_alone(1, 0)
        with pe.Fori(1, B) as b:
            expert_alone(1, b, lambda: turn_y(1, b - 1, ps_m))
        turn_y(1, B - 1, ps_m)

    @block.scalar
    def _(act):
        def high_queries_input(b):
            wait(act, xT_turned, b)
            wait(act, q_product, b - 1)
            act.activation(xhT[0][:], ps_y[:], ACT.Copy).then_inc(xT_hi.handle, 1)

        def bias_queries(b):
            wait(act, q_out, b - 1)
            for m in range(DC):
                wait(act, q_product, b, m + 1)
                act.activation(qf[:, m, :], ps_y[:, m, :], ACT.Identity, bias=bq[:, m:m + 1]).then_inc(q_biased.handle, 1)

        def probs(b, j):
            wait(act, s_shifted, b, j + 1)
            wait(act, p_turned, b if j >= 2 else b - 1, j - 1 if j >= 2 else j + 3)
            act.activation(pr[:, j % 2, :], sc[:, j % 2, :], ACT.Exp).then_inc(p_exp.handle, 1)

        def turned(b, j):
            wait(act, p_turned, b, j + 1)
            wait(act, o_product, b if j >= 2 else b - 1, j - 1 if j >= 2 else j + 3)
            act.activation(pT[:, j % 2, :], ps_l[:].rearrange("p a b -> p (a b)"), ACT.Copy).then_inc(pT_ready.handle, 1)

        def high_output(b):
            wait(act, o_turned, b)
            wait(act, a_product, b - 1)
            act.activation(oT[0], ps_s[:], ACT.Copy).then_inc(oT_hi.handle, 1)

        def copy_x2(b):
            wait(act, x2_turned, b)
            wait(act, x2T_out, b - 1)
            wait(act, r_product, b - 1)
            wait(act, ex[0]["x2_lo"], b - 1)
            act.activation(x2T, ps_s[:], ACT.Copy).then_inc(x2T_ready.handle, 1)

        def router_exp(b):
            wait(act, r_step, b)
            act.activation(lt[:], lg[:], ACT.Exp).then_inc(r_exp.handle, 1)

        def gelu(e, b, f):
            s = ex[e]
            wait(act, s["h_product"], b, f + 1)
            wait(act, s["g_lo"], b if f >= 4 else b - 1, f - 3 if f >= 4 else f + 5)
            act.activation(g[:, f % 4, :], ps_l[:, f % 2, :], ACT.Gelu_apprx_tanh,
                           bias=bias[:, e, f:f + 1]).then_inc(s["gelu"].handle, 1)
            wait(act, s["y_step"], b if f >= 4 else b - 1, f - 3 if f >= 4 else f + 5)
            act.activation(gs[0][:, f % 4, :], ps_l[:, f % 2, :], ACT.Gelu_apprx_tanh,
                           bias=bias[:, e, f:f + 1]).then_inc(s["g_hi"].handle, 1)

        def bias_y(e, b):
            s = ex[e]
            wait(act, s["y_step"], b)
            wait(act, s["y_turned"], b - 1)
            for m in range(DC):
                act.activation(yT[:, m, :], ps_y[:, m, :], ACT.Identity,
                               bias=bias[:, e, FC + m:FC + m + 1]).then_inc(s["y_biased"].handle, 1)

        act.wait_ge(ctx_turned, 1)
        act.activation(cT[0], ps_m[:], ACT.Copy).then_inc(ctx_hi, 1)
        high_queries_input(0)
        bias_queries(0)
        act.wait_ge(k_turned, 1)
        act.activation(kT[0], ps_m[:], ACT.Copy).then_inc(k_hi, 1)

        def body(i, rnd, first=False, last=False):
            if not first:
                router_exp(i - 1)
            probs(i, 0)
            probs(i, 1)
            turned(i, 0)
            probs(i, 2)
            turned(i, 1)
            if not last:
                high_queries_input(i + 1)
            probs(i, 3)
            turned(i, 2)
            turned(i, 3)
            if not last:
                bias_queries(i + 1)
            if not first:
                gelu(0, i - 1, 0)
                gelu(0, i - 1, 1)
            high_output(i)
            if not first:
                for f in range(2, 6):
                    gelu(0, i - 1, f)
            copy_x2(i)
            if not first:
                gelu(0, i - 1, 6)
                gelu(0, i - 1, 7)
                bias_y(0, i - 1)

        def last_expert():
            router_exp(B - 1)
            for f in range(FC):
                gelu(0, B - 1, f)
            bias_y(0, B - 1)

        pipeline(act, body, lambda: None, last_expert)
        act.wait_ge(pb_ready, 2)
        wait(act, ex[0]["g_lo"], B - 1)
        wait(act, ex[0]["y_step"], B - 1)
        wait(act, ex[0]["y_turned"], B - 1)
        with act.Fori(0, B) as b:
            for f in range(FC):
                gelu(1, b, f)
            bias_y(1, b)

    @block.gpsimd
    def _(pool):
        pool.memset(ident[:], 0.0).then_inc(consts_ready, 1)
        pool.wait_ge(consts_ready, 1)
        pool.affine_select(out=ident[:], in_=ident[:], compare_op=ALU.not_equal, fill=1.0, base=0,
                           pattern=[[-1, P]], channel_multiplier=1).then_inc(eye_ready, 1)
        pool.memset(ones[:], 1.0).then_inc(consts_ready, 1)
        pool.memset(ones_bf[:], 1.0).then_inc(consts_ready, 1)
        pool.memset(mhalf[:], -0.5).then_inc(consts_ready, 1)
        pool.memset(vbd[:], 0.0).then_inc(eye_ready, 1)
        pool.wait_ge(eye_ready, 2)
        root = float(DK) ** 0.5
        pool.memset(vbd[0:CT, :, 2 * DK:2 * DK + 1], root).then_inc(eye_ready, 1)
        pool.wait_ge(eye_ready, 3)
        pool.memset(vbd[CT:P, :, 2 * DK + 1:2 * DK + 2], root).then_inc(eye_ready, 1)
        pool.wait_ge(eye_ready, 4)
        for n in range(2):
            pool.memset(kbd[n][:].bitcast(F32), 0.0).then_inc(eye_ready, 1)

        def rsqrt(n, b):
            s = ln[n]
            wait(pool, s["var"], b)
            pool.tensor_tensor(rstd[n][:], var[n][:], mhalf[:], ALU.pow).then_inc(s["rstd"].handle, 1)
            wait(pool, s["rstd"], b)
            pool.tensor_tensor(shiftby[n][:], nmean[n][:], rstd[n][:], ALU.mult).then_inc(s["shift"].handle, 1)

        def normalise(n, b, src):
            s = ln[n]
            wait(pool, s["shift"], b)
            wait(pool, xT_turned if n == 0 else x2_turned, b - 1)
            pool.tensor_tensor(tick[:], mhalf[:, 0:1], mhalf[:, 0:1], ALU.add)
            for t in range(NT):
                pool.tensor_scalar(xh[n][:, t, :], src[:, t, :], rstd[n][:, t:t + 1], shiftby[n][:, t:t + 1],
                                   ALU.mult, ALU.add).then_inc(s["xhat"].handle, 1)

        def shift(b, j):
            wait(pool, s_max, b, j + 1)
            m = sc[:, j % 2, :].rearrange("p (h k) -> p h k", k=CT)
            pool.tensor_tensor(m, m, mx[:, j % 2, :].unsqueeze(2).to_broadcast([P, H, CT]), ALU.subtract).then_inc(s_shifted.handle, 1)

        def bias_residual(b):
            wait(pool, xr_in, b)
            for t in range(NT):
                i = pool.tensor_tensor(x2[:, t, :], x2[:, t, :], bpb, ALU.add)
            i.then_inc(xr_biased.handle, 1)

        def low_part(e, b, f):
            s = ex[e]
            wait(pool, s["g_hi"], b, f + 1)
            wait(pool, s["y_step"], b if f >= 4 else b - 1, f - 3 if f >= 4 else f + 5)
            pool.tensor_tensor(gs[1][:, f % 4, :], g[:, f % 4, :], gs[0][:, f % 4, :].bitcast(F32), ALU.subtract).then_inc(s["g_lo"].handle, 1)

        rsqrt(0, 0)
        normalise(0, 0, xa)

        def body(i, rnd, first=False, last=False):
            shift(i, 0)
            if not last:
                rsqrt(0, i + 1)
                normalise(0, i + 1, xa)
            shift(i, 1)
            shift(i, 2)
            bias_residual(i)
            shift(i, 3)
            if not first:
                for f in range(4):
                    low_part(0, i - 1, f)
            rsqrt(1, i)
            normalise(1, i, x2)
            if not first:
                for f in range(4, 6):
                    low_part(0, i - 1, f)
            rsqrt(2, i)
            if not first:
                for f in range(6, FC):
                    low_part(0, i - 1, f)

        def last_expert():
            for f in range(FC):
                low_part(0, B - 1, f)

        pipeline(pool, body, lambda: None, last_expert)

    @block.vector
    def _(dve):
        def split(dst, src, hi_signal, hi_value, lo_signal):
            dve.tensor_copy(dst[0], src).then_inc(hi_signal, 1)
            dve.wait_ge(hi_signal, hi_value)
            dve.tensor_tensor(dst[1], src, dst[0].bitcast(F32), ALU.subtract).then_inc(lo_signal, 1)

        def stats(n, b, src):
            s = ln[n]
            for t in range(NT):
                dve.bn_stats(stat[:, t, :], src[:, t, :]).then_inc(s["stats"].handle, 1)
            wait(dve, s["stats"], b)
            dve.memset(carry[:], 0.0)
            for t in range(NT):
                dve.bn_aggr(mv[n][:, t, :], stat[:, t, :]).then_inc(s["mean"].handle, 1)
            wait(dve, s["mean"], b)
            dve.tensor_scalar(var[n][:], mv[n][:, :, 1], EPS, None, ALU.add).then_inc(s["var"].handle, 1)
            dve.tensor_scalar(nmean[n][:], mv[n][:, :, 0], -1.0, None, ALU.mult).then_inc(s["var"].handle, 1)

        def low_queries_input(b):
            wait(dve, xT_hi, b)
            dve.tensor_tensor(xhT[1][:], ps_y[:], xhT[0][:].bitcast(F32), ALU.subtract).then_inc(xT_lo.handle, 1)

        def split_queries(b):
            wait(dve, q_in, b)
            wait(dve, s_product, b - 1)
            split([t[:] for t in qs], qr[:], q_hi.handle, q_hi.at(b), q_lo.handle)

        def mask_scores(b, j):
            m = sc[:, j % 2, :].rearrange("p (h k) -> p h k", k=CT)
            if j == 0:
                wait(dve, mask_in, b)
            wait(dve, s_product, b, j + 1)
            wait(dve, p_exp, b if j >= 2 else b - 1, j - 1 if j >= 2 else j + 3)
            dve.tensor_tensor(m, ps_s[:].rearrange("p a (h k) -> p (a h) k", k=CT),
                              mk[:, j, :].unsqueeze(1).to_broadcast([P, H, CT]), ALU.mult).then_inc(s_masked.handle, 1)
            wait(dve, s_masked, b, j + 1)
            wait(dve, s_shifted, b if j >= 2 else b - 1, j - 1 if j >= 2 else j + 3)
            dve.tensor_reduce(mx[:, j % 2, :], m, AX.X, ALU.max).then_inc(s_max.handle, 1)

        def normalise_output(b, j):
            o = ps_m[:, 0, 0:G * VW].rearrange("p (g v) -> p g v", v=VW)
            wait(dve, o_product, b, j + 1)
            dve.reciprocal(rs[:, j % 2, :].rearrange("p (g o) -> p g o", o=2), o[:, :, 2 * DK:VW]).then_inc(o_recip.handle, 1)
            wait(dve, o_recip, b, j + 1)
            if j == 0:
                wait(dve, o_turned, b - 1)
            for a in range(2):
                i = dve.tensor_tensor(
                    on[:, j, :].rearrange("p (g v) -> p g v", v=2 * DK)[:, :, a * DK:(a + 1) * DK],
                    o[:, :, a * DK:(a + 1) * DK],
                    rs[:, j % 2, :].rearrange("p (g o) -> p g o", o=2)[:, :, a:a + 1].to_broadcast([P, G, DK]), ALU.mult)
            i.then_inc(o_norm.handle, 1)

        def low_output(b):
            wait(dve, oT_hi, b)
            dve.tensor_tensor(oT[1], ps_s[:], oT[0].bitcast(F32), ALU.subtract).then_inc(oT_lo.handle, 1)

        def add_residual(b):
            wait(dve, xr_biased, b)
            for n in range(2):
                wait(dve, a_product, b, n + 1)
                half_x2 = x2[:, 2 * n:2 * n + 2, :].rearrange("p t d -> p (t d)")
                dve.tensor_tensor(half_x2, ps_s[:, n, :], half_x2, ALU.add).then_inc(x2_ready.handle, 1)
            wait(dve, x2_ready, b)

        def split_x2(e, b):
            s = ex[e]
            wait(dve, x2T_ready if e == 0 else xt_in, b)
            wait(dve, s["h_product"], b - 1)
            split([t[:] for t in x2s], x2T, s["x2_hi"].handle, s["x2_hi"].at(b), s["x2_lo"].handle)

        def over(ap):
            return ap.unsqueeze(2).to_broadcast([P, NT, E])

        def each(ap):
            return ap.unsqueeze(1).to_broadcast([P, NT, E])

        def logits(b):
            wait(dve, r_product, b)
            wait(dve, ln[2]["shift"], b)
            dve.tensor_tensor(lg[:], ps_m[:, 0, 0:NT * E].rearrange("p (t e) -> p t e", e=E), over(rstd[2][:]), ALU.mult).then_inc(r_step.handle, 1)
            dve.tensor_tensor(lt[:], each(rc[:, 0, :]), over(shiftby[2][:]), ALU.mult).then_inc(r_step.handle, 1)
            wait(dve, r_step, b, 2)
            dve.tensor_tensor(lg[:], lg[:], lt[:], ALU.add).then_inc(r_step.handle, 1)
            wait(dve, r_step, b, 3)
            dve.tensor_tensor(lg[:], lg[:], each(rc[:, 1, :]), ALU.add).then_inc(r_step.handle, 1)
            wait(dve, r_step, b, 4)
            dve.tensor_reduce(lmx[:], lg[:], AX.X, ALU.max).then_inc(r_step.handle, 1)
            wait(dve, r_step, b, 5)
            dve.tensor_tensor(lg[:], lg[:], over(lmx[:]), ALU.subtract).then_inc(r_step.handle, 1)

        def probabilities(b):
            wait(dve, r_exp, b)
            dve.tensor_reduce(s8[:], lt[:], AX.X, ALU.add).then_inc(r_sum.handle, 1)
            dve.tensor_reduce(s7[:], lt[:, :, 1:E], AX.X, ALU.add).then_inc(r_sum.handle, 1)
            wait(dve, r_sum, b, 2)
            dve.reciprocal(s8[:], s8[:]).then_inc(r_sum.handle, 1)
            wait(dve, r_sum, b)
            wait(dve, ex[0]["acc_io"], b - 1)
            dve.tensor_tensor(p0[:], lt[:, :, 0], s8[:], ALU.mult).then_inc(r_probs.handle, 1)
            dve.tensor_tensor(acc[:, :, D], s7[:], s8[:], ALU.mult).then_inc(r_probs.handle, 1)

        def mix(e, b, src):
            s = ex[e]
            wait(dve, s["y_turned"], b)
            if e == 0:
                wait(dve, r_probs, b)
                wait(dve, keep_in, b)
            else:
                wait(dve, s["acc_io"], b)
            for t in range(NT):
                weight = p0[:, t:t + 1] if e == 0 else acc[:, t, D:D + 1]
                base = keep[:, t, :] if e == 0 else acc[:, t, 0:D]
                dve.scalar_tensor_tensor(acc[:, t, 0:D], src[:, t // 2, (t % 2) * D:(t % 2) * D + D], weight, base,
                                         ALU.mult, ALU.add).then_inc(s["mixed"].handle, 1)

        def halfword(ap, upper):
            return ap.bitcast(U16).rearrange("p (n two) -> p n two", two=2)[:, :, upper]

        small = [(slice(0, FC), slice(0, FC)), (slice(FC, 2 * FC), slice(0, FC)),
                 (slice(2 * FC, 2 * FC + DC), slice(FC, FC + DC)), (slice(2 * FC + DC, 2 * (FC + DC)), slice(FC, FC + DC))]
        key_of = [[0, 0, 1, 1], [0, 2, 1, 3]]

        def compare(k, pair, rnd):
            if pair == 0:
                wait(dve, cand_step, k - 1)
            for s in (2 * pair, 2 * pair + 1):
                wait(dve, ind_counted, k if s >= 2 else k - 1, s - 1 if s >= 2 else s + 3)
                dve.tensor_scalar(ind[s % 2][:], key[:, key_of[rnd][s], :], cand[:, s:s + 1], None, ALU.is_le).then_inc(ind_ready.handle, 1)

        def counts(k):
            wait(dve, total_ready, k - 1)
            for s, (sk, _) in enumerate(small):
                dve.tensor_scalar(sind[:, sk], skey[:, sk], cand[:, 4 + s:5 + s], None, ALU.is_le, ALU.add,
                                  accum_out=cnt[:, 4 + s:5 + s]).then_inc(cnt_ready.handle, 1)
            wait(dve, ind_counted, k)
            dve.tensor_copy(cnt[:, 0:4], ps_m[:, 1, 0:4]).then_inc(cnt_ready.handle, 1)

        def decide(k):
            wait(dve, total_ready, k)
            totals = ps_m[:, 1, NS:2 * NS]
            dve.tensor_tensor(fail[:], totals, ranks[:], ALU.is_lt).then_inc(failed.handle, 1)
            wait(dve, failed, k)
            dve.tensor_tensor(fcnt[:], totals, fail[:], ALU.mult).then_inc(below_step.handle, 1)
            dve.scalar_tensor_tensor(prefix[:], fail[:], half[:, 0:1], prefix[:], ALU.mult, ALU.add).then_inc(prefix_step.handle, 1)
            wait(dve, prefix_step, k, 1)
            wait(dve, below_step, k)
            dve.tensor_scalar(half[:], half[:], 0.5, None, ALU.mult).then_inc(prefix_step.handle, 1)
            dve.tensor_tensor(below[:], below[:], fcnt[:], ALU.max)
            wait(dve, prefix_step, k)
            dve.tensor_scalar(cand[:], prefix[:], half[:, 0:1], 1.0, ALU.add, ALU.subtract).then_inc(cand_step.handle, 1)

        def start_round():
            dve.memset(prefix[:], 0.0).then_inc(state_ready, 1)
            dve.memset(below[:], 0.0).then_inc(state_ready, 1)
            dve.memset(half[:], float(2 ** (BITS - 1))).then_inc(state_ready, 1)
            dve.memset(cand[:], float(2 ** (BITS - 1) - 1)).then_inc(state_ready, 1)

        def second_round():
            wait(dve, cand_step, BITS - 1)
            wait(dve, ind_counted, BITS - 1)
            marks = 0
            for n in range(2):
                dve.wait_ge(key_ready, 8 + 2 * n)
                for s in range(2):
                    dve.tensor_scalar(ind[s][:].bitcast(U16), key[:, n, :], prefix[:, 2 * n + s:2 * n + s + 1], 65535.0,
                                      ALU.not_equal, ALU.mult).then_inc(key_mark, 1)
                marks += 2
                dve.wait_ge(key_mark, marks)
                dve.tensor_tensor(key[:, n, :], ind[0][:].bitcast(U16), key[:, 2 + n, :], ALU.max).then_inc(key_ready, 1)
                dve.tensor_tensor(key[:, 2 + n, :], ind[1][:].bitcast(U16), key[:, 2 + n, :], ALU.max).then_inc(key_ready, 1)
            for s, (sk, v) in enumerate(small):
                mark = sind[:, sk].bitcast(U16)
                dve.tensor_scalar(mark, skey[:, sk], prefix[:, 4 + s:5 + s], 65535.0, ALU.not_equal, ALU.mult).then_inc(key_mark, 1)
                marks += 1
                dve.wait_ge(key_mark, marks)
                dve.tensor_tensor(skey[:, sk], mark, halfword(bias[:, 0, v], 0), ALU.max).then_inc(key_ready, 1)
            dve.tensor_copy(thr[:, :, 1], prefix[:]).then_inc(thr_ready, 1)
            dve.tensor_tensor(ranks[:], ranks[:], below[:], ALU.subtract).then_inc(state_ready, 1)
            dve.wait_ge(thr_ready, 1)
            dve.wait_ge(state_ready, NS + 5)
            start_round()
            dve.wait_ge(state_ready, NS + 9)
            dve.wait_ge(key_ready, 16)

        dve.wait_ge(ld_w4, 64)
        split([w.rearrange("p n c d -> p (n c d)") for w in wkv], stage[:, DC * D:3 * DC * D], proj_hi, 1, proj_lo)
        for n, start in enumerate((0, 3 * DC * D)):
            split([w[:, n].rearrange("p c d -> p (c d)") for w in wqp], stage[:, start:start + DC * D], proj_hi, n + 2, proj_lo)
        dve.wait_ge(ctx_hi, 1)
        dve.tensor_tensor(cT[1], ps_m[:], cT[0].bitcast(F32), ALU.subtract).then_inc(ctx_lo, 1)
        wait(dve, x_in, 0)
        stats(0, 0, xa)
        dve.wait_ge(ld_small, 16 * 8)
        for n, (src, row) in enumerate(((ps_s, bkb), (ps_l, bvb))):
            dve.wait_ge(kv_product, (n + 1) * KC)
            for k in range(KC):
                dve.tensor_tensor(kv[:, n, k, :], src[:, k // 2, (k % 2) * D:(k % 2) * D + D], row, ALU.add).then_inc(kv_biased, 1)
        low_queries_input(0)
        for c in range(DC):
            dve.tensor_scalar(gw[:, c, :], wr[:, c, :], gam[:, c:c + 1], None, ALU.mult).then_inc(route_w, 1)
            dve.tensor_scalar(bw[:, c, :], wr[:, c, :], bet[:, c:c + 1], None, ALU.mult).then_inc(route_w, 1)
        dve.wait_ge(ld_w, 64)
        for n in range(2):
            dve.tensor_scalar(key[:, n, :], halfword(wraw[:, n, :], 1), 0x7FFF, None, ALU.bitwise_and).then_inc(key_ready, 1)
            dve.tensor_copy(key[:, 2 + n, :], halfword(wraw[:, n, :], 0)).then_inc(key_ready, 1)
        for sk, v in small:
            dve.tensor_scalar(skey[:, sk], halfword(bias[:, 0, v], 1), 0x7FFF, None, ALU.bitwise_and).then_inc(key_ready, 1)
        for n, ws in enumerate((w1s, w2s)):
            split([t[:] for t in ws], wraw[:, n, :], w_hi, n + 1, w_lo)
        dve.wait_ge(route_sum, 1)
        dve.tensor_copy(rc[:, 0, :], ps_s[:, 0, 0:E])
        dve.tensor_tensor(rc[:, 1, :], ps_s[:, 0, E:2 * E], brb[:], ALU.add).then_inc(route_ready, 1)
        dve.wait_ge(k_hi, 1)
        dve.tensor_tensor(kT[1], ps_m[:], kT[0].bitcast(F32), ALU.subtract).then_inc(k_lo, 1)
        for s, r in enumerate(RANKS):
            dve.memset(ranks[:, s:s + 1], float(r)).then_inc(state_ready, 1)
        start_round()
        split_queries(0)
        dve.wait_ge(state_ready, NS + 4)
        dve.wait_ge(key_ready, 8)

        def body(i, rnd, first=False, last=False):
            k = 4 * i
            compare(k, 0, rnd)
            mask_scores(i, 0)
            if not last:
                wait(dve, x_in, i + 1)
                stats(0, i + 1, xa)
            mask_scores(i, 1)
            compare(k, 1, rnd)
            mask_scores(i, 2)
            normalise_output(i, 0)
            counts(k)
            mask_scores(i, 3)
            decide(k)
            if not last:
                low_queries_input(i + 1)
            normalise_output(i, 1)
            compare(k + 1, 0, rnd)
            normalise_output(i, 2)
            normalise_output(i, 3)
            compare(k + 1, 1, rnd)
            if not first:
                probabilities(i - 1)
            counts(k + 1)
            decide(k + 1)
            low_output(i)
            compare(k + 2, 0, rnd)
            add_residual(i)
            stats(1, i, x2)
            compare(k + 2, 1, rnd)
            counts(k + 2)
            decide(k + 2)
            wait(dve, ln[1]["xhat"], i)
            stats(2, i, xh[1])
            compare(k + 3, 0, rnd)
            compare(k + 3, 1, rnd)
            if not last:
                split_queries(i + 1)
            counts(k + 3)
            decide(k + 3)
            split_x2(0, i)
            logits(i)
            if not first:
                mix(0, i - 1, ps_s)

        def last_expert():
            probabilities(B - 1)
            finish_search()
            mix(0, B - 1, ps_s)
            finish_weights()

        steps = [0]

        def perturb(dst, w, mag, tr, s, done):
            limit = thr[:].rearrange("p s two -> p (s two)").bitcast(F32)

            def after(ins):
                steps[0] += 1
                ins.then_inc(tier_step, 1)
                dve.wait_ge(tier_step, steps[0])
            after(dve.tensor_scalar(mag.bitcast(U32), w.bitcast(U32), 0x7FFFFFFF, None, ALU.bitwise_and))
            after(dve.tensor_scalar(tr, mag, limit[:, s:s + 1], -2.0, ALU.is_ge, ALU.mult))
            after(dve.scalar_tensor_tensor(tr, mag, limit[:, s + 1:s + 2], tr, ALU.is_le, ALU.add))
            after(dve.tensor_scalar(tr, tr, -1.0, SCALE, ALU.max, ALU.mult))
            after(dve.tensor_tensor(tr, tr, w, ALU.mult))
            dve.tensor_tensor(dst, tr, w, ALU.add).then_inc(done, 1)

        def finish_search():
            wait(dve, cand_step, 2 * BITS - 1)
            dve.tensor_copy(thr[:, :, 0], prefix[:]).then_inc(thr_ready, 1)
            dve.wait_ge(thr_ready, 2)
            dve.wait_ge(ld_again, 32)
            mag = key[:, 0:2].rearrange("p a n -> p (a n)").bitcast(F32)
            for n in range(2):
                perturb(wagain[:, n, :], wagain[:, n, :], mag, tier, 2 * n, pw_ready)
            for part, s in ((slice(0, FC), 4), (slice(FC, FC + DC), 6)):
                perturb(bias[:, 1, part], bias[:, 0, part], sabs[:, part], tier[:, part], s, pb_ready)

        def finish_weights():
            dve.wait_ge(pw_ready, 2)
            for n, ws in enumerate((w1s, w2s)):
                wait(dve, ex[0]["h_product"] if n == 0 else ex[0]["y_step"], B - 1)
                split([t[:] for t in ws], wagain[:, n, :], pw_hi, n + 1, pw_lo)

        pipeline(dve, body, second_round, last_expert)

        def perturbed_expert(b, first=False):
            split_x2(1, b)
            s = ex[1]
            for f in range(FC):
                if f == 2 and not first:
                    mix(1, b - 1, ps_m)
                wait(dve, s["g_hi"], b, f + 1)
                wait(dve, s["y_step"], b if f >= 4 else b - 1, f - 3 if f >= 4 else f + 5)
                dve.tensor_tensor(gs[1][:, f % 4, :], g[:, f % 4, :], gs[0][:, f % 4, :].bitcast(F32), ALU.subtract).then_inc(s["g_lo"].handle, 1)

        perturbed_expert(0, first=True)
        with dve.Fori(1, B) as b:
            perturbed_expert(b)
        mix(1, B - 1, ps_m)

    ctx.close()


_INS = ["x", "ctx_1024", "mask_BxSxS2_ff1", "L0_xattn_WQ", "L0_xattn_bQ", "L0_xattn_WK", "L0_xattn_bK",
        "L0_xattn_WV", "L0_xattn_bV", "L0_xattn_Wp", "L0_xattn_bp", "L0_ffn_W1", "L0_ffn_b1", "L0_ffn_W2",
        "L0_ffn_b2", "L0_ffn_ln_gamma", "L0_ffn_ln_beta", "L0_ffn_Wr", "L0_ffn_br"]


def kernel(**inputs):
    import numpy as np
    import concourse.bacc as bacc
    from concourse.bass_utils import run_bass_kernel_spmd

    nc = bacc.Bacc("TRN2", target_bir_lowering=False, num_devices=1)
    arrays, args = {}, []
    for name in _INS:
        a = np.ascontiguousarray(inputs[name])
        arrays["in_" + name] = a
        args.append(nc.dram_tensor("in_" + name, a.shape, mybir.dt.from_np(a.dtype), kind="ExternalInput").ap())
    args.append(nc.dram_tensor("out_x", inputs["x"].shape, F32, kind="ExternalOutput").ap())
    build_program(nc, *args)
    return run_bass_kernel_spmd(nc, [arrays], core_ids=[0]).results[0]["out_x"]
```

```python
from contextlib import ExitStack

import concourse.bass as bass
from concourse import mybir

ALU = mybir.AluOpType
ACT = mybir.ActivationFunctionType
AX = mybir.AxisListType
F32 = mybir.dt.float32
F32R = mybir.dt.float32r
BF16 = mybir.dt.bfloat16
U16 = mybir.dt.uint16
U32 = mybir.dt.uint32

P = 128
EPS = 1e-5
SPARSITY = 0.1
SCALE = 0.8
BITS = (15, 16)
AHEAD = 3


class Signal:

    def __init__(self, handle, per):
        self.handle, self.per = handle, per

    def at(self, batch, count=None):
        return (batch + 1) * self.per + (self.per if count is None else count)


def build_program(nc, x, ctx_in, mask, WQ, bQ, WK, bK, WV, bV, Wp, bp,
                  W1, b1, W2, b2, gamma, beta, Wr, br, out):
    B, S, D = x.shape
    CT = ctx_in.shape[1]
    F = W1.shape[1]
    E = Wr.shape[1]
    H = 16
    DK = D // H
    NT = S // P
    DC = D // P
    FC = F // P
    HH = H // 2
    R = S // H
    C = S // R
    G = H // 2
    VW = 2 * DK + 2
    KC = B * CT // P
    assert (P, DC, R * C, HH * DK, 2 * CT, HH * CT) == (128, 2, S, P, P, 512)

    def rank(n, top):
        k = max(1, int(n * SPARSITY / 2))
        return n - k + 1 if top else k
    SEARCH_N = [D * F, D * F, D * F, D * F, F, F, D, D]
    RANKS = [rank(n, s % 2 == 0) for s, n in enumerate(SEARCH_N)]
    NS = len(RANKS)
    WN = D * F // P

    ctx = ExitStack()

    def sb(name, shape, dt=F32):
        return ctx.enter_context(nc.sbuf_tensor(name, shape, dt))

    def sig(name, per=1):
        s = Signal(ctx.enter_context(nc.semaphore(name)), per)
        signals.append(s)
        return s

    def sem(name):
        return ctx.enter_context(nc.semaphore(name))

    signals = []

    ps_s, ps_l, ps_y, ps_m = (ctx.enter_context(nc.psum_tensor(f"ps_{n}", [P, 2, 512], F32)) for n in "slym")

    q_scr = nc.dram_tensor("q_scr", [B, H, DK, C, R], F32, kind="Internal").ap()
    v_scr = nc.dram_tensor("v_scr", [B, CT, D], F32, kind="Internal").ap()
    k_scr = nc.dram_tensor("k_scr", [B, CT, D], F32, kind="Internal").ap()
    kh_scr = nc.dram_tensor("kh_scr", [B, P, 2 * DC * CT], F32, kind="Internal").ap()
    xt_scr = nc.dram_tensor("xt_scr", [B, P, DC * S], F32, kind="Internal").ap()
    acc_scr = nc.dram_tensor("acc_scr", [B, P, NT * (D + 1)], F32, kind="Internal").ap()

    def view(region, start, *shape):
        n = 1
        for d in shape:
            n *= d
        ap = region[:, start:start + n]
        if len(shape) == 1:
            return ap
        names = "abc"[:len(shape)]
        return ap.rearrange("p (" + " ".join(names) + ") -> p " + " ".join(names), **dict(zip(names[1:], shape[1:])))

    region_a = sb("region_a", [P, 6 * H * CT])
    region_b = sb("region_b", [P, 2 * WN])
    region_c = [sb(f"region_c_{n}", [P, 4 * S], F32R) for n in ("hi", "lo")]
    region_d = [sb(f"region_d_{n}", [P, DC * S], F32R) for n in ("hi", "lo")]
    stage = view(region_a, 0, 4 * DC * D)
    ctxt = view(region_a, 4 * DC * D, KC, D)
    kv = view(region_a, 4 * DC * D + KC * D, 2, KC, D)
    kk = view(region_a, 4 * DC * D + 3 * KC * D, KC, D)
    sc = view(region_a, 0, 2, H * CT)
    pr = view(region_a, 2 * H * CT, 2, H * CT)
    pT = view(region_a, 4 * H * CT, 2, G * P)
    wraw = view(region_b, 0, 2, WN)
    x2T = view(region_b, 0, DC, S)
    yT = view(region_b, DC * S, DC, S)
    g = view(region_b, 2 * DC * S, 4, S)
    wagain = view(region_a, 0, 2, WN)
    tier = view(region_a, 2 * WN, WN)
    cT = [view(r, 0, DC, B * CT) for r in region_c]
    kT = [view(r, DC * B * CT, DC, B * CT) for r in region_c]
    gs = [view(r, 0, 4, S) for r in region_c]
    wkv = [view(r, 0, 2, DC, D) for r in region_d]
    oT = [view(r, 0, DC, S) for r in region_d]

    ident = sb("ident", [P, P])
    ones = sb("ones", [P, P])
    ones_bf = sb("ones_bf", [P, 2], BF16)
    mhalf = sb("mhalf", [P, NT])
    epsb = sb("epsb", [P, NT])
    wqp = [sb(f"wqp_{n}", [P, 2, DC, D], F32R) for n in ("hi", "lo")]
    bq = sb("bq", [P, DC])
    rows = sb("rows", [P, 3, D])
    bkb, bvb, bpb = (rows[:, n, :] for n in range(3))
    w1s = [sb(f"w1_{n}", [P, DC * F], F32R) for n in ("hi", "lo")]
    w2s = [sb(f"w2_{n}", [P, FC * D], F32R) for n in ("hi", "lo")]
    bias = sb("bias", [P, 2, FC + DC])
    gam = sb("gam", [P, DC])
    bet = sb("bet", [P, DC])
    wr = sb("wr", [P, DC, E])
    gw = sb("gw", [P, DC, E])
    bw = sb("bw", [P, DC, E])
    brb = sb("brb", [P, E])
    rc = sb("rc", [P, E])

    key = sb("key", [P, 4, WN], U16)
    skey = sb("skey", [P, 2 * (FC + DC)], U16)
    ind = [sb(f"ind{n}", [P, WN], BF16) for n in range(2)]
    sind = sb("sind", [P, 2 * (FC + DC)], BF16)
    sabs = sb("sabs", [P, FC + DC])
    ranks = sb("ranks", [P, NS])
    prefix = sb("prefix", [P, NS])
    cand = sb("cand", [P, NS])
    half = sb("half", [P, 1])
    below = sb("below", [P, NS])
    cnt = sb("cnt", [P, NS])
    fail = sb("fail", [P, NS])
    fcnt = sb("fcnt", [P, NS])
    thr = sb("thr", [P, NS, 2], U16)

    xa = sb("xa", [P, NT, D])
    x2 = sb("x2", [P, NT, D])
    keep = sb("keep", [P, NT, D])
    mk = sb("mk", [P, NT, CT])
    stat = sb("stat", [P, NT, 6])
    mv = [sb(f"mv{n}", [P, NT, 2]) for n in range(2)]
    var = [sb(f"var{n}", [P, NT]) for n in range(2)]
    rstd = [sb(f"rstd{n}", [P, NT]) for n in range(2)]
    nmean = [sb(f"nmean{n}", [P, NT]) for n in range(2)]
    shiftby = [sb(f"shiftby{n}", [P, NT]) for n in range(2)]
    rvar = sb("rvar", [P, NT])
    rrstd = sb("rrstd", [P, NT])
    carry = sb("carry", [P, 1])
    tick = sb("tick", [P, 1])
    xh = [sb(f"xh{n}", [P, NT, D]) for n in range(2)]
    xhT = [sb(f"xhT_{n}", [P, DC, S], F32R) for n in ("hi", "lo")]
    qf = sb("qf", [P, DC, S])
    qr = sb("qr", [P, DC, S])
    qs = [sb(f"qs_{n}", [P, DC, S], F32R) for n in ("hi", "lo")]
    kbd = sb("kbd", [P, 2, DC, HH, CT], F32R)
    vbd = sb("vbd", [P, G, VW])
    mx = sb("mx", [P, 2, H])
    rs = sb("rs", [P, 2, H])
    on = sb("on", [P, NT, D])

    x2s = [sb(f"x2s_{n}", [P, DC, S], F32R) for n in ("hi", "lo")]
    lg = sb("lg", [P, NT, E])
    lt = sb("lt", [P, NT, E])
    lmx = sb("lmx", [P, NT])
    s8 = sb("s8", [P, NT])
    s7 = sb("s7", [P, NT])
    p0 = sb("p0", [P, NT])
    acc = sb("acc", [P, NT, D + 1])

    ld_w4 = [sem(f"ld_w{n}") for n in "qkvp"]
    ld_bq = sem("ld_bq")
    ld_route = sem("ld_route")
    ld_row = [sem(f"ld_row_{n}") for n in ("bk", "bv", "bp")]
    ld_ctx = sem("ld_ctx")
    ld_w = sem("ld_w12")
    ld_again = sem("ld_again")
    consts_ready = sem("consts_ready")
    eye_ready = sem("eye_ready")
    proj_hi = [sem(f"proj_hi_{n}") for n in "qkvp"]
    proj_lo = [sem(f"proj_lo_{n}") for n in "qkvp"]
    ctx_turned = sem("ctx_turned")
    ctx_hi = sem("ctx_hi")
    ctx_lo = sem("ctx_lo")
    kv_product = sem("kv_product")
    kv_biased = sem("kv_biased")
    kv_out = sem("kv_out")
    kk_in = sem("kk_in")
    k_turned = sem("k_turned")
    k_hi = sem("k_hi")
    k_lo = sem("k_lo")
    kh_out = sem("kh_out")
    w_hi = sem("w_hi")
    w_lo = sem("w_lo")
    route_w = sem("route_w")
    route_sum = sem("route_sum")
    route_ready = sem("route_ready")
    key_ready = sem("key_ready")
    state_ready = sem("state_ready")
    key_mark = sem("key_mark")
    thr_ready = sem("thr_ready")
    tier_step = sem("tier_step")
    pw_ready = sem("pw_ready")
    pw_hi = sem("pw_hi")
    pw_lo = sem("pw_lo")
    pb_ready = sem("pb_ready")

    ind_ready = sig("ind_ready", 4)
    ind_counted = sig("ind_counted", 4)
    cnt_ready = sig("cnt_ready", 5)
    total_ready = sig("total_ready")
    failed = sig("failed")
    below_step = sig("below_step")
    prefix_step = sig("prefix_step", 2)
    cand_step = sig("cand_step")

    x_in = sig("x_in", 16)
    xr_in = sig("xr_in", 16)
    keep_in = sig("keep_in", 16)
    mask_in = sig("mask_in", 16)
    v_in = sig("v_in", 32)
    k_in = sig("k_in", 16 * HH)
    q_out = sig("q_out", 16 * DC)
    q_in = sig("q_in", 16)
    ln = [dict(stats=sig(f"ln{n}_stats", NT), mean=sig(f"ln{n}_mean", NT), var=sig(f"ln{n}_var", 2),
               rstd=sig(f"ln{n}_rstd"), shift=sig(f"ln{n}_shift"), xhat=sig(f"ln{n}_xhat", NT)) for n in range(2)]
    xT_turned = sig("xT_turned")
    xT_hi = sig("xT_hi")
    xT_lo = sig("xT_lo")
    q_product = sig("q_product", DC)
    q_biased = sig("q_biased", DC)
    q_hi = sig("q_hi", DC)
    q_lo = sig("q_lo", DC)
    s_product = sig("s_product", NT * DC)
    s_masked = sig("s_masked", NT * DC)
    s_max = sig("s_max", NT)
    s_shifted = sig("s_shifted", NT)
    p_exp = sig("p_exp", NT)
    p_turned = sig("p_turned", NT)
    pT_ready = sig("pT_ready", NT)
    o_product = sig("o_product", NT)
    o_recip = sig("o_recip", NT)
    o_norm = sig("o_norm", NT)
    o_turned = sig("o_turned")
    oT_hi = sig("oT_hi")
    oT_lo = sig("oT_lo")
    a_product = sig("a_product", 2)
    xr_biased = sig("xr_biased")
    x2_ready = sig("x2_ready", 2)
    x2_turned = sig("x2_turned")
    x2T_ready = sig("x2T_ready")
    x2T_out = sig("x2T_out", 16)
    r_product = sig("r_product")
    r_var = sig("r_var", 3)
    r_rstd = sig("r_rstd")
    r_step = sig("r_step", 4)
    r_exp = sig("r_exp")
    r_sum = sig("r_sum", 3)
    r_probs = sig("r_probs", 2)

    ex = [dict(
        x2_hi=sig(f"e{e}_x2_hi"), x2_lo=sig(f"e{e}_x2_lo"),
        h_product=sig(f"e{e}_h_product", FC), gelu=sig(f"e{e}_gelu", FC),
        g_hi=sig(f"e{e}_g_hi", FC), g_lo=sig(f"e{e}_g_lo", FC),
        y_step=sig(f"e{e}_y_step", FC), y_biased=sig(f"e{e}_y_biased", DC),
        y_turned=sig(f"e{e}_y_turned"), mixed=sig(f"e{e}_mixed", NT),
        acc_io=sig(f"e{e}_acc_io", 16), out_io=sig(f"e{e}_out_io", 16)) for e in range(2)]
    xt_in = sig("xt_in", 16)

    def tiles(ap):
        return ap.rearrange("(p j) d -> p j d", j=NT)

    def after(b):
        return b + 1 if not isinstance(b, int) or b + 1 < B else b

    def three(eng, out_ap, a, b, first=True, last=True):
        eng.matmul(out_ap, a[0], b[0], start=first, stop=False)
        eng.matmul(out_ap, a[0], b[1], start=False, stop=False)
        return eng.matmul(out_ap, a[1], b[0], start=False, stop=last)

    turned_in = [ps_l] * (NT - 1) + [ps_y]

    def by_tile(m):
        return (qr[:, m, :].rearrange("q (cc j r) -> q j r cc", r=R, j=NT),
                [t[:, m, :].rearrange("q (j r cc) -> q j r cc", r=R, j=NT) for t in qs])

    def wait(eng, signal, batch, count=None):
        value = signal.at(batch, count)
        if not (isinstance(value, int) and value <= 0):
            eng.wait_ge(signal.handle, value)

    with nc.Block() as credit:
        @credit.gpsimd
        def _(pool):
            for s in signals:
                pool.sem_inc(s.handle, s.per)

    SWITCH = (BITS[0] - AHEAD) // 4
    assert AHEAD + 4 * SWITCH == BITS[0] and 3 * (B - SWITCH) + 1 == BITS[1]

    def step_of(i, rnd):
        return (AHEAD + 4 * i) if rnd == 0 else (BITS[0] - 3 * SWITCH) + 3 * i

    def pipeline(eng, body, between, last_expert):
        body(0, 0, first=True)
        with eng.Fori(1, SWITCH) as i:
            body(i, 0)
        between()
        with eng.Fori(SWITCH, B - 2) as i:
            body(i, 1)
        body(B - 2, 1)
        body(B - 1, 1, last=True)
        last_expert()

    block = ctx.enter_context(nc.Block())

    @block.sync
    def _(sp):
        def load_x(b):
            wait(sp, ln[0]["xhat"], b - 1)
            sp.dma_start(xa[:], tiles(x[b])).then_inc(x_in.handle, 16)

        def load_residual(b):
            wait(sp, ln[1]["xhat"], b - 1)
            wait(sp, keep_in, b - 1)
            sp.dma_start(x2[:], tiles(x[b])).then_inc(xr_in.handle, 16)

        def store_queries(b):
            wait(sp, q_biased, b)
            for m in range(DC):
                sp.dma_start(q_scr[b].rearrange("h d c r -> (d c) h r")[m * P:(m + 1) * P],
                             qf[:, m, :].rearrange("p (h r) -> p h r", r=R)).then_inc(q_out.handle, 16)

        def load_queries(b):
            wait(sp, q_out, b)
            wait(sp, q_lo, b - 1)
            sp.dma_start(qr[:], q_scr[b].rearrange("h d c r -> (h d) (c r)").rearrange("(m p) s -> p m s", p=P)).then_inc(q_in.handle, 16)

        def load_context(b):
            wait(sp, s_product, b - 1)
            for h in range(HH):
                sp.dma_start(kbd[DK * h:DK * h + DK, :, :, h, :].rearrange("p n c k -> p (n c) k").bitcast(F32),
                             kh_scr[b, DK * h:DK * h + DK].rearrange("p (n k) -> p n k", k=CT)).then_inc(k_in.handle, 16)
            wait(sp, s_masked, b - 1)
            sp.dma_start(mk[:], tiles(mask[b])).then_inc(mask_in.handle, 16)
            wait(sp, o_product, b - 1)
            for o in range(2):
                sp.dma_start(vbd[CT * o:CT * o + CT, :, DK * o:DK * o + DK],
                             v_scr[b].rearrange("t (c d) -> (t c) d", d=DK).rearrange("(g o k) d -> o k g d", k=CT, o=2)[o]).then_inc(v_in.handle, 16)

        def load_w(n, w):
            sp.dma_start(view(region_a, n * DC * D, DC, D), w.rearrange("(c p) n -> p c n", p=P)).then_inc(ld_w4[n], 16)

        def load_row(n, v):
            sp.dma_start(rows[:, n, :], v.rearrange("(a d) -> a d", a=1).to_broadcast([P, D])).then_inc(ld_row[n], 16)

        with nc.allow_non_contiguous_dma(reason="small vectors laid out by partition"):
            sp.dma_start(ctxt[:], ctx_in.rearrange("b t d -> (b t) d").rearrange("(k p) d -> p k d", p=P)).then_inc(ld_ctx, 16)
            load_w(1, WK)
            load_row(0, bK)
            load_w(2, WV)
            load_x(0)
            load_row(1, bV)
            load_w(0, WQ)
            for m in range(DC):
                sp.dma_start(bq[:, m:m + 1], bQ.rearrange("(c d a) -> d c a", d=DK, a=1)[m * (DK // DC):(m + 1) * (DK // DC)]).then_inc(ld_bq, 16)
            sp.dma_start(wraw[:, 0].rearrange("p (c f) -> p c f", c=DC), W1.rearrange("(c p) f -> p c f", p=P)).then_inc(ld_w, 16)
            sp.dma_start(bias[:, 0, 0:FC], b1.rearrange("(c p) -> p c", p=P)).then_inc(ld_w, 16)
            sp.dma_start(bias[:, 0, FC:FC + DC], b2.rearrange("(c p) -> p c", p=P)).then_inc(ld_w, 16)
            sp.dma_start(wraw[:, 1].rearrange("p (c d) -> p c d", c=FC), W2.rearrange("(c p) d -> p c d", p=P)).then_inc(ld_w, 16)
            load_row(2, bp)
            load_w(3, Wp)
            sp.dma_start(gam[:], gamma.rearrange("(c p) -> p c", p=P)).then_inc(ld_route, 16)
            sp.dma_start(bet[:], beta.rearrange("(c p) -> p c", p=P)).then_inc(ld_route, 16)
            sp.dma_start(wr[:], Wr.rearrange("(c p) e -> p c e", p=P)).then_inc(ld_route, 16)
            sp.dma_start(brb[:], br.rearrange("(a e) -> a e", a=1).to_broadcast([P, E])).then_inc(ld_route, 16)
        sp.wait_ge(kv_biased, KC)
        sp.dma_start(k_scr.rearrange("b t d -> (b t) d").rearrange("(k p) d -> p k d", p=P), kv[:, 0]).then_inc(kv_out, 16)
        load_x(1)
        sp.wait_ge(kv_out, 16)
        for b in range(B):
            sp.dma_start(kk[CT * (b % 2):CT * (b % 2) + CT, b // 2].rearrange("k (h d) -> k h d", d=DK),
                         k_scr[b].rearrange("t (c d) -> (t c) d", d=DK).rearrange("(h k) d -> k h d", k=CT)).then_inc(kk_in, 16)
        sp.wait_ge(kv_biased, 2 * KC)
        sp.dma_start(v_scr.rearrange("b t d -> (b t) d").rearrange("(k p) d -> p k d", p=P), kv[:, 1]).then_inc(kv_out, 16)
        store_queries(0)
        sp.wait_ge(k_lo, 1)
        for n in range(2):
            for c in range(DC):
                sp.dma_start(kh_scr.rearrange("b p (n c k) -> n c p b k", n=2, c=DC)[n, c],
                             kT[n][:, c].rearrange("p (b k) -> p b k", k=CT).bitcast(F32)).then_inc(kh_out, 16)
        load_queries(0)
        sp.wait_ge(kh_out, 16 * 2 * DC)
        sp.wait_ge(kv_out, 32)
        sp.wait_ge(eye_ready, 5)
        load_context(0)

        def put_expert(b):
            wait(sp, ex[0]["mixed"], b)
            sp.dma_start(acc_scr[b], acc[:].rearrange("p t d -> p (t d)")).then_inc(ex[0]["acc_io"].handle, 16)

        def body(i, rnd, first=False, last=False):
            if not isinstance(i, int) or i + 2 < B:
                load_x(i + 2)
            load_residual(i)
            if not last:
                store_queries(i + 1)
                load_queries(i + 1)
                load_context(i + 1)
            else:
                wait(sp, o_product, i)
                sp.dma_start(wagain[:, 0].rearrange("p (c f) -> p c f", c=DC), W1.rearrange("(c p) f -> p c f", p=P)).then_inc(ld_again, 16)
                sp.dma_start(wagain[:, 1].rearrange("p (c d) -> p c d", c=FC), W2.rearrange("(c p) d -> p c d", p=P)).then_inc(ld_again, 16)
            wait(sp, x2T_ready, i)
            sp.dma_start(xt_scr[i], x2T.rearrange("p c s -> p (c s)")).then_inc(x2T_out.handle, 16)
            wait(sp, x2_ready, i)
            wait(sp, ex[0]["mixed"], i - 1)
            sp.dma_start(keep[:], x2[:]).then_inc(keep_in.handle, 16)
            if not first:
                put_expert(i - 1)

        def last_expert():
            wait(sp, x2T_out, B - 1)
            load_batch(0)
            put_expert(B - 1)

        s = ex[1]

        def load_batch(b):
            if isinstance(b, int):
                wait(sp, ex[0]["x2_lo"], B - 1)
                wait(sp, r_product, B - 1)
            else:
                wait(sp, s["x2_lo"], b - 1)
            sp.dma_start(x2T.rearrange("p c s -> p (c s)"), xt_scr[b]).then_inc(xt_in.handle, 16)

        def load_acc(b):
            wait(sp, s["out_io"], b - 1)
            sp.dma_start(acc[:].rearrange("p t d -> p (t d)"), acc_scr[b]).then_inc(s["acc_io"].handle, 16)

        def store(b):
            wait(sp, s["mixed"], b)
            sp.dma_start(tiles(out[b]), acc[:, :, 0:D]).then_inc(s["out_io"].handle, 16)

        pipeline(sp, body, lambda: None, last_expert)
        wait(sp, ex[0]["acc_io"], B - 1)
        load_acc(0)
        with sp.Fori(1, B) as b:
            load_batch(b)
            store(b - 1)
            load_acc(b)
        store(B - 1)
        wait(sp, ex[1]["out_io"], B - 1)

    @block.tensor
    def _(pe):
        def w_of(n, c, cols):
            return [w[:, n, c, cols] for w in wqp]

        def rows_of(t, c):
            return t[:, c, :].rearrange("q (j p) -> q p j", p=P)

        def turn_queries_input(b):
            wait(pe, ln[0]["xhat"], b)
            wait(pe, ex[0]["mixed"], b - 3)
            for c in range(DC):
                for t in range(NT):
                    mm = pe.transpose(ps_y[:, c, t * P:(t + 1) * P], xh[0][:, t, c * P:(c + 1) * P], ident[:])
            mm.then_inc(xT_turned.handle, 1)

        def queries(b):
            wait(pe, xT_hi, b)
            wait(pe, xT_lo, b)
            for m in range(DC):
                for c in range(DC):
                    mm = three(pe, ps_y[:, m, :], w_of(0, c, slice(m * P, (m + 1) * P)),
                               [rows_of(t, c) for t in xhT], c == 0, c == DC - 1)
                mm.then_inc(q_product.handle, 1)

        def scores(b, j):
            if j == 0:
                wait(pe, q_hi, b)
                wait(pe, q_lo, b)
                wait(pe, k_in, b)
                wait(pe, x2T_ready, b - 1)
            for m in range(DC):
                if j:
                    wait(pe, s_masked, b, DC * (j - 1) + m + 1)
                three(pe, ps_s[:, m, :], [t[:, m, j * P:(j + 1) * P] for t in qs],
                      [kbd[:, n, m].rearrange("p h k -> p (h k)") for n in range(2)]).then_inc(s_product.handle, 1)

        def turn_probs(b, j):
            wait(pe, p_exp, b, j + 1)
            if j == 0:
                wait(pe, ex[0]["g_hi"], b - 2)
            elif j < NT - 1:
                wait(pe, pT_ready, b, j)
            else:
                wait(pe, q_biased, after(b))
                wait(pe, ex[0]["mixed"], b - 2)
            dst = turned_in[j]
            for n in range(G):
                mm = pe.transpose(dst[:, n // 4, (n % 4) * P:(n % 4 + 1) * P], pr[:, j % 2, n * P:(n + 1) * P], ident[:])
            mm.then_inc(p_turned.handle, 1)

        def values(b, j):
            wait(pe, pT_ready, b, j + 1)
            if j == 0:
                wait(pe, v_in, b)
                wait(pe, r_step, b - 1, 1)
            else:
                wait(pe, o_norm, b, j)
            for n in range(G):
                mm = pe.matmul(ps_m[:, 0, n * VW:(n + 1) * VW], pT[:, j % 2, n * P:(n + 1) * P], vbd[:, n, :],
                               start=True, stop=True)
            mm.then_inc(o_product.handle, 1)

        def turn_output(b):
            wait(pe, o_norm, b)
            wait(pe, s_masked, b)
            for c in range(DC):
                for t in range(NT):
                    mm = pe.transpose(ps_s[:, c, t * P:(t + 1) * P], on[:, t, c * P:(c + 1) * P], ident[:])
            mm.then_inc(o_turned.handle, 1)

        def project(b):
            wait(pe, oT_hi, b)
            wait(pe, oT_lo, b)
            for t in range(NT):
                for c in range(DC):
                    mm = three(pe, ps_s[:, t // 2, (t % 2) * D:(t % 2) * D + D],
                               [o[:, c, t * P:(t + 1) * P] for o in oT], w_of(1, c, slice(0, D)), c == 0, c == DC - 1)
                if t % 2:
                    mm.then_inc(a_product.handle, 1)

        def turn_x2(b):
            wait(pe, ln[1]["xhat"], b)
            wait(pe, x2_ready, b)
            for c in range(DC):
                for t in range(NT):
                    mm = pe.transpose(ps_s[:, c, t * P:(t + 1) * P], xh[1][:, t, c * P:(c + 1) * P], ident[:])
            mm.then_inc(x2_turned.handle, 1)

        def router(b):
            wait(pe, x2T_ready, b)
            for t in range(NT):
                for c in range(DC):
                    mm = pe.matmul(ps_m[:, 0, t * E:(t + 1) * E], x2T[:, c, t * P:(t + 1) * P], gw[:, c, :],
                                   start=c == 0, stop=c == DC - 1)
            mm.then_inc(r_product.handle, 1)

        def hidden(e, b, f):
            s = ex[e]
            if f == 0:
                wait(pe, s["x2_hi"], b)
                wait(pe, s["x2_lo"], b)
                if e == 0:
                    wait(pe, pT_ready, after(b), NT - 1)
            if f >= 2:
                wait(pe, s["g_hi"], b, f - 1)
            elif e == 1:
                wait(pe, s["g_hi"], b - 1)
            for c in range(DC):
                mm = three(pe, ps_l[:, f % 2, :], [w[:, c * F + f * P:c * F + (f + 1) * P] for w in w1s],
                           [t[:, c, :] for t in x2s], c == 0, c == DC - 1)
            mm.then_inc(s["h_product"].handle, 1)

        def output(e, b, f):
            s = ex[e]
            if f == 0:
                wait(pe, s["y_biased"], b - 1)
                if e == 0:
                    wait(pe, s["mixed"], b - 1)
                    wait(pe, pT_ready, after(b))
            wait(pe, s["g_lo"], b, f + 1)
            for m in range(DC):
                mm = three(pe, ps_y[:, m, :], [w[:, f * D + m * P:f * D + (m + 1) * P] for w in w2s],
                           [t[:, f % 4, :] for t in gs], f == 0, f == FC - 1)
            mm.then_inc(s["y_step"].handle, 1)

        def turn_y(e, b, dst):
            s = ex[e]
            wait(pe, s["y_biased"], b)
            wait(pe, s["mixed"], b - 1)
            for t in range(NT):
                for c in range(DC):
                    mm = pe.transpose(dst[:, t // 2, (t % 2) * D + c * P:(t % 2) * D + (c + 1) * P],
                                      yT[:, c, t * P:(t + 1) * P], ident[:])
            mm.then_inc(s["y_turned"].handle, 1)

        def count(k, pair):
            for s in (2 * pair, 2 * pair + 1):
                wait(pe, ind_ready, k, s + 1)
                if s == 0:
                    wait(pe, below_step, k - 1)
                for c in range(WN // P):
                    mm = pe.matmul(ps_m[:, 1, s:s + 1], ind[s % 2][:, c * P:(c + 1) * P], ones_bf[:, 0:1],
                                   start=c == 0, stop=c == WN // P - 1)
                mm.then_inc(ind_counted.handle, 1)

        def total(k):
            wait(pe, cnt_ready, k)
            pe.matmul(ps_m[:, 1, NS:2 * NS], ones[:], cnt[:], start=True, stop=True).then_inc(total_ready.handle, 1)

        def keys_values(n, dst):
            pe.wait_ge(proj_lo[n + 1], 1)
            for k in range(KC):
                for c in range(DC):
                    mm = three(pe, dst[:, k // 2, (k % 2) * D:(k % 2) * D + D],
                               [t[:, c, k * P:(k + 1) * P] for t in cT], [w[:, n, c, :] for w in wkv],
                               c == 0, c == DC - 1)
                mm.then_inc(kv_product, 1)

        def step(k):
            count(k, 0)
            count(k, 1)
            total(k)

        pe.wait_ge(ld_ctx, 16)
        pe.wait_ge(eye_ready, 1)
        for c in range(DC):
            for k in range(KC):
                mm = pe.transpose(ps_m[:, c, k * P:(k + 1) * P], ctxt[:, k, c * P:(c + 1) * P], ident[:])
        mm.then_inc(ctx_turned, 1)
        pe.wait_ge(ctx_lo, 1)
        keys_values(0, ps_s)
        turn_queries_input(0)
        keys_values(1, ps_l)
        pe.wait_ge(proj_lo[0], 1)
        queries(0)
        pe.wait_ge(kk_in, 16 * B)
        for c in range(DC):
            for k in range(KC):
                mm = pe.transpose(ps_s[:, c, k * P:(k + 1) * P], kk[:, k, c * P:(c + 1) * P], ident[:])
        mm.then_inc(k_turned, 1)
        pe.wait_ge(consts_ready, 5)
        for k in range(AHEAD):
            step(k)
        pe.wait_ge(route_w, 2 * DC)
        for c in range(DC):
            mm = pe.matmul(ps_m[:, 0, 0:E], ones[:], bw[:, c, :], start=c == 0, stop=c == DC - 1)
        mm.then_inc(route_sum, 1)
        pe.wait_ge(proj_lo[3], 1)
        pe.wait_ge(k_lo, 1)
        scores(0, 0)
        scores(0, 1)
        scores(0, 2)
        pe.wait_ge(route_ready, 1)

        def body(i, rnd, first=False, last=False):
            k = step_of(i, rnd)
            more = not isinstance(i, int) or i + 2 < B
            turn_probs(i, 0)
            scores(i, 3)
            values(i, 0)
            if not last:
                turn_queries_input(i + 1)
            turn_probs(i, 1)
            count(k, 0)
            if not last:
                queries(i + 1)
            values(i, 1)
            count(k, 1)
            turn_probs(i, 2)
            turn_probs(i, 3)
            total(k)
            values(i, 2)

            def h(f):
                if not first:
                    if f == 0:
                        pe.wait_ge(w_lo, 2)
                    hidden(0, i - 1, f)

            def o(f):
                if not first:
                    output(0, i - 1, f)
            h(0)
            values(i, 3)
            h(1)
            turn_output(i)
            count(k + 1, 0)
            h(2)
            o(0)
            project(i)
            count(k + 1, 1)
            h(3)
            total(k + 1)
            o(1)
            h(4)
            o(2)
            count(k + 2, 0)
            h(5)
            count(k + 2, 1)
            turn_x2(i)
            total(k + 2)
            o(3)
            if rnd == 0 or last:
                count(k + 3, 0)
            h(6)
            if rnd == 0 or last:
                count(k + 3, 1)
                total(k + 3)
            if not last:
                scores(i + 1, 0)
            o(4)
            h(7)
            router(i)
            o(5)
            if not last:
                scores(i + 1, 1)
            o(6)
            o(7)
            if not last:
                scores(i + 1, 2)
            if not first:
                turn_y(0, i - 1, ps_y)

        def expert_alone(e, b, before_turn=None):
            for f in range(FC):
                hidden(e, b, f)
                if f == 1 and before_turn is not None:
                    before_turn()
                if f == 3 and e == 1 and isinstance(b, int):
                    pe.wait_ge(pw_lo, 2)
                if f >= 3:
                    output(e, b, f - 3)
            for f in range(FC - 3, FC):
                output(e, b, f)

        def last_expert():
            expert_alone(0, B - 1)
            turn_y(0, B - 1, ps_s)

        pipeline(pe, body, lambda: None, last_expert)
        pe.wait_ge(pw_lo, 1)
        wait(pe, ex[0]["g_hi"], B - 1)
        expert_alone(1, 0)
        with pe.Fori(1, B) as b:
            expert_alone(1, b, lambda: turn_y(1, b - 1, ps_m))
        turn_y(1, B - 1, ps_m)

    @block.scalar
    def _(act):
        def high_queries_input(b):
            wait(act, xT_turned, b)
            wait(act, q_product, b - 1)
            act.activation(xhT[0][:], ps_y[:], ACT.Copy).then_inc(xT_hi.handle, 1)

        def bias_queries(b):
            wait(act, q_out, b - 1)
            for m in range(DC):
                wait(act, q_product, b, m + 1)
                act.activation(qf[:, m, :], ps_y[:, m, :], ACT.Identity, bias=bq[:, m:m + 1]).then_inc(q_biased.handle, 1)

        def probs(b, j):
            wait(act, s_shifted, b, j + 1)
            wait(act, p_turned, b if j >= 2 else b - 1, j - 1 if j >= 2 else j + 3)
            act.activation(pr[:, j % 2, :], sc[:, j % 2, :], ACT.Exp).then_inc(p_exp.handle, 1)

        def turned(b, j):
            wait(act, p_turned, b, j + 1)
            wait(act, o_product, b if j >= 2 else b - 1, j - 1 if j >= 2 else j + 3)
            act.activation(pT[:, j % 2, :], turned_in[j][:].rearrange("p a b -> p (a b)"), ACT.Copy).then_inc(pT_ready.handle, 1)

        def high_output(b):
            wait(act, o_turned, b)
            wait(act, a_product, b - 1)
            act.activation(oT[0], ps_s[:], ACT.Copy).then_inc(oT_hi.handle, 1)

        def copy_x2(b):
            wait(act, x2_turned, b)
            wait(act, x2T_out, b - 1)
            wait(act, r_product, b - 1)
            wait(act, ex[0]["x2_lo"], b - 1)
            act.activation(x2T, ps_s[:], ACT.Copy).then_inc(x2T_ready.handle, 1)

        def router_exp(b):
            wait(act, r_step, b)
            act.activation(lt[:], lg[:], ACT.Exp).then_inc(r_exp.handle, 1)

        def gelu(e, b, f):
            s = ex[e]
            wait(act, s["h_product"], b, f + 1)
            wait(act, s["g_lo"], b if f >= 4 else b - 1, f - 3 if f >= 4 else f + 5)
            act.activation(g[:, f % 4, :], ps_l[:, f % 2, :], ACT.Gelu_apprx_tanh,
                           bias=bias[:, e, f:f + 1]).then_inc(s["gelu"].handle, 1)
            wait(act, s["y_step"], b if f >= 4 else b - 1, f - 3 if f >= 4 else f + 5)
            act.activation(gs[0][:, f % 4, :], ps_l[:, f % 2, :], ACT.Gelu_apprx_tanh,
                           bias=bias[:, e, f:f + 1]).then_inc(s["g_hi"].handle, 1)

        def bias_y(e, b):
            s = ex[e]
            wait(act, s["y_step"], b)
            wait(act, s["y_turned"], b - 1)
            for m in range(DC):
                act.activation(yT[:, m, :], ps_y[:, m, :], ACT.Identity,
                               bias=bias[:, e, FC + m:FC + m + 1]).then_inc(s["y_biased"].handle, 1)

        def high_queries(b):
            wait(act, q_in, b)
            wait(act, s_product, b - 1)
            for m in range(DC):
                src, dst = by_tile(m)
                act.activation(dst[0], src, ACT.Copy).then_inc(q_hi.handle, 1)

        def high_x2(b):
            wait(act, x2T_ready, b)
            wait(act, ex[0]["h_product"], b - 1)
            act.activation(x2s[0][:], x2T, ACT.Copy).then_inc(ex[0]["x2_hi"].handle, 1)

        act.wait_ge(ctx_turned, 1)
        act.activation(cT[0], ps_m[:], ACT.Copy).then_inc(ctx_hi, 1)
        high_queries_input(0)
        act.wait_ge(ld_bq, 16 * DC)
        bias_queries(0)
        act.wait_ge(k_turned, 1)
        act.activation(kT[0], ps_s[:], ACT.Copy).then_inc(k_hi, 1)
        high_queries(0)
        act.wait_ge(ld_w, 64)
        for n, ws in enumerate((w1s, w2s)):
            act.activation(ws[0][:], wraw[:, n, :], ACT.Copy).then_inc(w_hi, 1)
        probs(0, 0)
        probs(0, 1)

        def body(i, rnd, first=False, last=False):
            turned(i, 0)
            if not last:
                high_queries_input(i + 1)
            probs(i, 2)
            turned(i, 1)
            if not last:
                bias_queries(i + 1)
            probs(i, 3)
            turned(i, 2)
            turned(i, 3)
            if not first:
                gelu(0, i - 1, 0)
            high_output(i)
            if not first:
                for f in range(1, 5):
                    gelu(0, i - 1, f)
            if not last:
                high_queries(i + 1)
            if first:
                act.wait_ge(w_lo, 2)
                act.wait_ge(key_ready, 8)
            else:
                gelu(0, i - 1, 5)
            copy_x2(i)
            if not first:
                gelu(0, i - 1, 6)
                gelu(0, i - 1, 7)
            high_x2(i)
            router_exp(i)
            if not last:
                probs(i + 1, 0)
            if not first:
                bias_y(0, i - 1)
            if not last:
                probs(i + 1, 1)

        def last_expert():
            for f in range(FC):
                gelu(0, B - 1, f)
            bias_y(0, B - 1)

        pipeline(act, body, lambda: None, last_expert)
        act.wait_ge(pb_ready, 2)
        wait(act, ex[0]["g_lo"], B - 1)
        wait(act, ex[0]["y_step"], B - 1)
        wait(act, ex[0]["y_turned"], B - 1)
        with act.Fori(0, B) as b:
            for f in range(FC):
                gelu(1, b, f)
            bias_y(1, b)

    @block.gpsimd
    def _(pool):
        pool.memset(ident[:], 0.0).then_inc(consts_ready, 1)
        pool.wait_ge(consts_ready, 1)
        pool.affine_select(out=ident[:], in_=ident[:], compare_op=ALU.not_equal, fill=1.0, base=0,
                           pattern=[[-1, P]], channel_multiplier=1).then_inc(eye_ready, 1)
        pool.memset(ones[:], 1.0).then_inc(consts_ready, 1)
        pool.memset(ones_bf[:], 1.0).then_inc(consts_ready, 1)
        pool.memset(mhalf[:], -0.5).then_inc(consts_ready, 1)
        pool.memset(epsb[:], EPS).then_inc(consts_ready, 1)
        pool.memset(vbd[:], 0.0).then_inc(eye_ready, 1)
        pool.wait_ge(eye_ready, 2)
        root = float(DK) ** 0.5
        pool.memset(vbd[0:CT, :, 2 * DK:2 * DK + 1], root).then_inc(eye_ready, 1)
        pool.wait_ge(eye_ready, 3)
        pool.memset(vbd[CT:P, :, 2 * DK + 1:2 * DK + 2], root).then_inc(eye_ready, 1)
        pool.wait_ge(eye_ready, 4)
        pool.memset(kbd[:].rearrange("p n c h k -> p (n c h k)").bitcast(F32), 0.0).then_inc(eye_ready, 1)

        def rsqrt(n, b):
            s = ln[n]
            wait(pool, s["var"], b)
            pool.tensor_tensor(rstd[n][:], var[n][:], mhalf[:], ALU.pow).then_inc(s["rstd"].handle, 1)
            wait(pool, s["rstd"], b)
            pool.tensor_tensor(shiftby[n][:], nmean[n][:], rstd[n][:], ALU.mult).then_inc(s["shift"].handle, 1)

        def normalise(n, b, src):
            s = ln[n]
            wait(pool, s["shift"], b)
            wait(pool, xT_turned if n == 0 else x2_turned, b - 1)
            pool.tensor_tensor(tick[:], mhalf[:, 0:1], mhalf[:, 0:1], ALU.add)
            for t in range(NT):
                pool.tensor_scalar(xh[n][:, t, :], src[:, t, :], rstd[n][:, t:t + 1], shiftby[n][:, t:t + 1],
                                   ALU.mult, ALU.add).then_inc(s["xhat"].handle, 1)

        def shift(b, j):
            wait(pool, s_max, b, j + 1)
            m = sc[:, j % 2, :].rearrange("p (h k) -> p h k", k=CT)
            pool.tensor_tensor(m, m, mx[:, j % 2, :].unsqueeze(2).to_broadcast([P, H, CT]), ALU.subtract).then_inc(s_shifted.handle, 1)

        def router_rsqrt(b):
            wait(pool, r_step, b - 1, 1)
            pool.tensor_tensor(rvar[:], rstd[1][:], rstd[1][:], ALU.mult).then_inc(r_var.handle, 1)
            wait(pool, r_var, b, 1)
            pool.tensor_tensor(rvar[:], rvar[:], mv[1][:, :, 1], ALU.mult).then_inc(r_var.handle, 1)
            wait(pool, r_var, b, 2)
            pool.tensor_tensor(rvar[:], rvar[:], epsb[:], ALU.add).then_inc(r_var.handle, 1)
            wait(pool, r_var, b)
            pool.tensor_tensor(rrstd[:], rvar[:], mhalf[:], ALU.pow).then_inc(r_rstd.handle, 1)

        def bias_residual(b):
            wait(pool, xr_in, b)
            for t in range(NT):
                i = pool.tensor_tensor(x2[:, t, :], x2[:, t, :], bpb, ALU.add)
            i.then_inc(xr_biased.handle, 1)

        def low_part(e, b, f):
            s = ex[e]
            wait(pool, s["g_hi"], b, f + 1)
            wait(pool, s["y_step"], b if f >= 4 else b - 1, f - 3 if f >= 4 else f + 5)
            pool.tensor_tensor(gs[1][:, f % 4, :], g[:, f % 4, :], gs[0][:, f % 4, :].bitcast(F32), ALU.subtract).then_inc(s["g_lo"].handle, 1)

        rsqrt(0, 0)
        normalise(0, 0, xa)
        for n, ws in enumerate((w1s, w2s)):
            pool.wait_ge(w_hi, n + 1)
            pool.tensor_tensor(ws[1][:], wraw[:, n, :], ws[0][:].bitcast(F32), ALU.subtract).then_inc(w_lo, 1)
        rsqrt(0, 1)
        normalise(0, 1, xa)
        pool.wait_ge(ld_row[2], 16)
        shift(0, 0)
        shift(0, 1)
        shift(0, 2)

        def body(i, rnd, first=False, last=False):
            shift(i, 3)
            bias_residual(i)
            if not first:
                for f in range(3):
                    low_part(0, i - 1, f)
            rsqrt(1, i)
            normalise(1, i, x2)
            if not first:
                for f in range(3, FC - 1):
                    low_part(0, i - 1, f)
            router_rsqrt(i)
            if not last:
                shift(i + 1, 0)
            if not first:
                low_part(0, i - 1, FC - 1)
            if not last:
                shift(i + 1, 1)
            if not isinstance(i, int) or i + 2 < B:
                rsqrt(0, i + 2)
                normalise(0, i + 2, xa)
            if not last:
                shift(i + 1, 2)

        def last_expert():
            for f in range(FC):
                low_part(0, B - 1, f)

        pipeline(pool, body, lambda: None, last_expert)

    @block.vector
    def _(dve):
        def split(dst, src, hi_signal, hi_value, lo_signal):
            dve.tensor_copy(dst[0], src).then_inc(hi_signal, 1)
            dve.wait_ge(hi_signal, hi_value)
            dve.tensor_tensor(dst[1], src, dst[0].bitcast(F32), ALU.subtract).then_inc(lo_signal, 1)

        def stats(n, b, src):
            s = ln[n]
            for t in range(NT):
                dve.bn_stats(stat[:, t, :], src[:, t, :]).then_inc(s["stats"].handle, 1)
            wait(dve, s["stats"], b)
            dve.memset(carry[:], 0.0)
            for t in range(NT):
                dve.bn_aggr(mv[n][:, t, :], stat[:, t, :]).then_inc(s["mean"].handle, 1)
            wait(dve, s["mean"], b)
            dve.tensor_scalar(var[n][:], mv[n][:, :, 1], EPS, None, ALU.add).then_inc(s["var"].handle, 1)
            dve.tensor_scalar(nmean[n][:], mv[n][:, :, 0], -1.0, None, ALU.mult).then_inc(s["var"].handle, 1)

        def low_queries_input(b):
            wait(dve, xT_hi, b)
            dve.tensor_tensor(xhT[1][:], ps_y[:], xhT[0][:].bitcast(F32), ALU.subtract).then_inc(xT_lo.handle, 1)

        def low_queries(b):
            wait(dve, q_hi, b)
            for m in range(DC):
                src, dst = by_tile(m)
                dve.tensor_tensor(dst[1], src, dst[0].bitcast(F32), ALU.subtract).then_inc(q_lo.handle, 1)

        def low_x2(b):
            wait(dve, ex[0]["x2_hi"], b)
            dve.tensor_tensor(x2s[1][:], x2T, x2s[0][:].bitcast(F32), ALU.subtract).then_inc(ex[0]["x2_lo"].handle, 1)

        def mask_scores(b, j):
            m = sc[:, j % 2, :].rearrange("p (h k) -> p h k", k=CT)
            if j == 0:
                wait(dve, mask_in, b)
            wait(dve, p_exp, b if j >= 2 else b - 1, j - 1 if j >= 2 else j + 3)
            for n in range(DC):
                wait(dve, s_product, b, DC * j + n + 1)
                dve.tensor_tensor(m[:, n * HH:(n + 1) * HH], ps_s[:, n, :].rearrange("p (h k) -> p h k", k=CT),
                                  mk[:, j, :].unsqueeze(1).to_broadcast([P, HH, CT]), ALU.mult).then_inc(s_masked.handle, 1)
            wait(dve, s_masked, b, DC * (j + 1))
            wait(dve, s_shifted, b if j >= 2 else b - 1, j - 1 if j >= 2 else j + 3)
            dve.tensor_reduce(mx[:, j % 2, :], m, AX.X, ALU.max).then_inc(s_max.handle, 1)

        def normalise_output(b, j):
            o = ps_m[:, 0, 0:G * VW].rearrange("p (g v) -> p g v", v=VW)
            wait(dve, o_product, b, j + 1)
            dve.reciprocal(rs[:, j % 2, :].rearrange("p (g o) -> p g o", o=2), o[:, :, 2 * DK:VW]).then_inc(o_recip.handle, 1)
            wait(dve, o_recip, b, j + 1)
            if j == 0:
                wait(dve, o_turned, b - 1)
            for a in range(2):
                i = dve.tensor_tensor(
                    on[:, j, :].rearrange("p (g v) -> p g v", v=2 * DK)[:, :, a * DK:(a + 1) * DK],
                    o[:, :, a * DK:(a + 1) * DK],
                    rs[:, j % 2, :].rearrange("p (g o) -> p g o", o=2)[:, :, a:a + 1].to_broadcast([P, G, DK]), ALU.mult)
            i.then_inc(o_norm.handle, 1)

        def low_output(b):
            wait(dve, oT_hi, b)
            dve.tensor_tensor(oT[1], ps_s[:], oT[0].bitcast(F32), ALU.subtract).then_inc(oT_lo.handle, 1)

        def add_residual(b):
            wait(dve, xr_biased, b)
            for n in range(2):
                wait(dve, a_product, b, n + 1)
                half_x2 = x2[:, 2 * n:2 * n + 2, :].rearrange("p t d -> p (t d)")
                dve.tensor_tensor(half_x2, ps_s[:, n, :], half_x2, ALU.add).then_inc(x2_ready.handle, 1)
            wait(dve, x2_ready, b)

        def split_x2(b):
            wait(dve, xt_in, b)
            if isinstance(b, int) and b == 0:
                wait(dve, ex[0]["h_product"], B - 1)
            else:
                wait(dve, ex[1]["h_product"], b - 1)
            split([t[:] for t in x2s], x2T, ex[1]["x2_hi"].handle, ex[1]["x2_hi"].at(b), ex[1]["x2_lo"].handle)

        def over(ap):
            return ap.unsqueeze(2).to_broadcast([P, NT, E])

        def logits(b):
            wait(dve, r_product, b)
            wait(dve, r_rstd, b)
            dve.tensor_tensor(lg[:], ps_m[:, 0, 0:NT * E].rearrange("p (t e) -> p t e", e=E), over(rrstd[:]), ALU.mult).then_inc(r_step.handle, 1)
            wait(dve, r_step, b, 1)
            dve.tensor_tensor(lg[:], lg[:], rc[:].unsqueeze(1).to_broadcast([P, NT, E]), ALU.add).then_inc(r_step.handle, 1)
            wait(dve, r_step, b, 2)
            dve.tensor_reduce(lmx[:], lg[:], AX.X, ALU.max).then_inc(r_step.handle, 1)
            wait(dve, r_step, b, 3)
            dve.tensor_tensor(lg[:], lg[:], over(lmx[:]), ALU.subtract).then_inc(r_step.handle, 1)

        def probabilities(b):
            wait(dve, r_exp, b)
            dve.tensor_reduce(s8[:], lt[:], AX.X, ALU.add).then_inc(r_sum.handle, 1)
            dve.tensor_reduce(s7[:], lt[:, :, 1:E], AX.X, ALU.add).then_inc(r_sum.handle, 1)
            wait(dve, r_sum, b, 2)
            dve.reciprocal(s8[:], s8[:]).then_inc(r_sum.handle, 1)
            wait(dve, r_sum, b)
            wait(dve, ex[0]["acc_io"], b - 1)
            dve.tensor_tensor(p0[:], lt[:, :, 0], s8[:], ALU.mult).then_inc(r_probs.handle, 1)
            dve.tensor_tensor(acc[:, :, D], s7[:], s8[:], ALU.mult).then_inc(r_probs.handle, 1)

        def mix(e, b, src):
            s = ex[e]
            wait(dve, s["y_turned"], b)
            if e == 0:
                wait(dve, r_probs, b)
                wait(dve, keep_in, b)
            else:
                wait(dve, s["acc_io"], b)
            for t in range(NT):
                weight = p0[:, t:t + 1] if e == 0 else acc[:, t, D:D + 1]
                base = keep[:, t, :] if e == 0 else acc[:, t, 0:D]
                dve.scalar_tensor_tensor(acc[:, t, 0:D], src[:, t // 2, (t % 2) * D:(t % 2) * D + D], weight, base,
                                         ALU.mult, ALU.add).then_inc(s["mixed"].handle, 1)

        def halfword(ap, upper):
            return ap.bitcast(U16).rearrange("p (n two) -> p n two", two=2)[:, :, upper]

        small = [(slice(0, FC), slice(0, FC)), (slice(FC, 2 * FC), slice(0, FC)),
                 (slice(2 * FC, 2 * FC + DC), slice(FC, FC + DC)), (slice(2 * FC + DC, 2 * (FC + DC)), slice(FC, FC + DC))]
        key_of = [[0, 0, 1, 1], [0, 2, 1, 3]]

        def compare(k, pair, rnd):
            if pair == 0:
                wait(dve, cand_step, k - 1)
            for s in (2 * pair, 2 * pair + 1):
                wait(dve, ind_counted, k if s >= 2 else k - 1, s - 1 if s >= 2 else s + 3)
                dve.tensor_scalar(ind[s % 2][:], key[:, key_of[rnd][s], :], cand[:, s:s + 1], None, ALU.is_le).then_inc(ind_ready.handle, 1)

        def counts(k):
            wait(dve, total_ready, k - 1)
            for s, (sk, _) in enumerate(small):
                dve.tensor_scalar(sind[:, sk], skey[:, sk], cand[:, 4 + s:5 + s], None, ALU.is_le, ALU.add,
                                  accum_out=cnt[:, 4 + s:5 + s]).then_inc(cnt_ready.handle, 1)
            wait(dve, ind_counted, k)
            dve.tensor_copy(cnt[:, 0:4], ps_m[:, 1, 0:4]).then_inc(cnt_ready.handle, 1)

        def decide(k):
            wait(dve, total_ready, k)
            totals = ps_m[:, 1, NS:2 * NS]
            dve.tensor_tensor(fail[:], totals, ranks[:], ALU.is_lt).then_inc(failed.handle, 1)
            wait(dve, failed, k)
            dve.tensor_tensor(fcnt[:], totals, fail[:], ALU.mult).then_inc(below_step.handle, 1)
            dve.scalar_tensor_tensor(prefix[:], fail[:], half[:, 0:1], prefix[:], ALU.mult, ALU.add).then_inc(prefix_step.handle, 1)
            wait(dve, prefix_step, k, 1)
            wait(dve, below_step, k)
            dve.tensor_scalar(half[:], half[:], 0.5, None, ALU.mult).then_inc(prefix_step.handle, 1)
            dve.tensor_tensor(below[:], below[:], fcnt[:], ALU.max)
            wait(dve, prefix_step, k)
            dve.tensor_scalar(cand[:], prefix[:], half[:, 0:1], 1.0, ALU.add, ALU.subtract).then_inc(cand_step.handle, 1)

        def start_round(bits):
            dve.memset(prefix[:], 0.0).then_inc(state_ready, 1)
            dve.memset(below[:], 0.0).then_inc(state_ready, 1)
            dve.memset(half[:], float(2 ** (bits - 1))).then_inc(state_ready, 1)
            dve.memset(cand[:], float(2 ** (bits - 1) - 1)).then_inc(state_ready, 1)

        def second_round():
            wait(dve, cand_step, BITS[0] - 1)
            wait(dve, ind_counted, BITS[0] - 1)
            marks = 0
            for n in range(2):
                dve.wait_ge(key_ready, 8 + 2 * n)
                for s in range(2):
                    dve.tensor_scalar(ind[s][:].bitcast(U16), key[:, n, :], prefix[:, 2 * n + s:2 * n + s + 1], 65535.0,
                                      ALU.not_equal, ALU.mult).then_inc(key_mark, 1)
                marks += 2
                dve.wait_ge(key_mark, marks)
                dve.tensor_tensor(key[:, n, :], ind[0][:].bitcast(U16), key[:, 2 + n, :], ALU.max).then_inc(key_ready, 1)
                dve.tensor_tensor(key[:, 2 + n, :], ind[1][:].bitcast(U16), key[:, 2 + n, :], ALU.max).then_inc(key_ready, 1)
            for s, (sk, v) in enumerate(small):
                mark = sind[:, sk].bitcast(U16)
                dve.tensor_scalar(mark, skey[:, sk], prefix[:, 4 + s:5 + s], 65535.0, ALU.not_equal, ALU.mult).then_inc(key_mark, 1)
                marks += 1
                dve.wait_ge(key_mark, marks)
                dve.tensor_tensor(skey[:, sk], mark, halfword(bias[:, 0, v], 0), ALU.max).then_inc(key_ready, 1)
            dve.tensor_copy(thr[:, :, 1], prefix[:]).then_inc(thr_ready, 1)
            dve.tensor_tensor(ranks[:], ranks[:], below[:], ALU.subtract).then_inc(state_ready, 1)
            dve.wait_ge(thr_ready, 1)
            dve.wait_ge(state_ready, NS + 5)
            start_round(BITS[1])
            dve.wait_ge(state_ready, NS + 9)
            dve.wait_ge(key_ready, 16)

        def step(k, rnd):
            compare(k, 0, rnd)
            compare(k, 1, rnd)
            counts(k)
            decide(k)

        def split_projection(n, dst):
            dve.wait_ge(ld_w4[n], 16)
            src = stage[:, n * DC * D:(n + 1) * DC * D].rearrange("p (c d) -> p c d", d=D)
            if n == 0:
                src = src.rearrange("p c (h d) -> p c d h", d=DK)
                dst = [w.rearrange("p c (d h) -> p c d h", d=DK) for w in dst]
            for c in range(DC):
                dve.tensor_copy(dst[0][:, c], src[:, c]).then_inc(proj_hi[n], 1)
            dve.wait_ge(proj_hi[n], DC)
            for c in range(DC):
                i = dve.tensor_tensor(dst[1][:, c], src[:, c], dst[0][:, c].bitcast(F32), ALU.subtract)
            i.then_inc(proj_lo[n], 1)

        def bias_context(n, src, row):
            dve.wait_ge(ld_row[n], 16)
            for k in range(KC):
                dve.wait_ge(kv_product, n * KC + 2 * (k // 2) + 2)
                dve.tensor_tensor(kv[:, n, k, :], src[:, k // 2, (k % 2) * D:(k % 2) * D + D], row, ALU.add).then_inc(kv_biased, 1)

        split_projection(1, [w[:, 0] for w in wkv])
        dve.wait_ge(ctx_hi, 1)
        dve.tensor_tensor(cT[1], ps_m[:], cT[0].bitcast(F32), ALU.subtract).then_inc(ctx_lo, 1)
        split_projection(2, [w[:, 1] for w in wkv])
        wait(dve, x_in, 0)
        stats(0, 0, xa)
        split_projection(0, [w[:, 0] for w in wqp])
        bias_context(0, ps_s, bkb)
        split_projection(3, [w[:, 1] for w in wqp])
        low_queries_input(0)
        bias_context(1, ps_l, bvb)
        dve.wait_ge(ld_w, 64)
        for n in range(2):
            dve.tensor_scalar(key[:, n, :], halfword(wraw[:, n, :], 1), 0x7FFF, None, ALU.bitwise_and).then_inc(key_ready, 1)
        for sk, v in small:
            dve.tensor_scalar(skey[:, sk], halfword(bias[:, 0, v], 1), 0x7FFF, None, ALU.bitwise_and).then_inc(key_ready, 1)
        for s, r in enumerate(RANKS):
            dve.memset(ranks[:, s:s + 1], float(r)).then_inc(state_ready, 1)
        start_round(BITS[0])
        dve.wait_ge(state_ready, NS + 4)
        dve.wait_ge(key_ready, 6)
        compare(0, 0, 0)
        dve.wait_ge(k_hi, 1)
        dve.tensor_tensor(kT[1], ps_s[:], kT[0].bitcast(F32), ALU.subtract).then_inc(k_lo, 1)
        compare(0, 1, 0)
        counts(0)
        decide(0)
        for k in range(1, AHEAD - 1):
            step(k, 0)
        dve.wait_ge(ld_route, 64)
        for c in range(DC):
            dve.tensor_scalar(bw[:, c, :], wr[:, c, :], bet[:, c:c + 1], None, ALU.mult).then_inc(route_w, 1)
            dve.tensor_scalar(gw[:, c, :], wr[:, c, :], gam[:, c:c + 1], None, ALU.mult).then_inc(route_w, 1)
        low_queries(0)
        wait(dve, x_in, 1)
        stats(0, 1, xa)
        step(AHEAD - 1, 0)
        dve.wait_ge(route_sum, 1)
        dve.tensor_tensor(rc[:], ps_m[:, 0, 0:E], brb[:], ALU.add).then_inc(route_ready, 1)
        mask_scores(0, 0)
        mask_scores(0, 1)
        mask_scores(0, 2)

        def body(i, rnd, first=False, last=False):
            k = step_of(i, rnd)
            more = not isinstance(i, int) or i + 2 < B
            mask_scores(i, 3)
            normalise_output(i, 0)
            compare(k, 0, rnd)
            if not last:
                low_queries_input(i + 1)
            compare(k, 1, rnd)
            normalise_output(i, 1)
            counts(k)
            decide(k)
            if first:
                for n in range(2):
                    dve.tensor_copy(key[:, 2 + n, :], halfword(wraw[:, n, :], 0)).then_inc(key_ready, 1)
            compare(k + 1, 0, rnd)
            normalise_output(i, 2)
            normalise_output(i, 3)
            if not first:
                probabilities(i - 1)
            low_output(i)
            compare(k + 1, 1, rnd)
            counts(k + 1)
            add_residual(i)
            stats(1, i, x2)
            decide(k + 1)
            compare(k + 2, 0, rnd)
            compare(k + 2, 1, rnd)
            counts(k + 2)
            if not last:
                low_queries(i + 1)
            decide(k + 2)
            if rnd == 0 or last:
                step(k + 3, rnd)
            if more:
                wait(dve, x_in, i + 2)
                stats(0, i + 2, xa)
            if not last:
                mask_scores(i + 1, 0)
            logits(i)
            if not last:
                mask_scores(i + 1, 1)
            low_x2(i)
            if not last:
                mask_scores(i + 1, 2)
            if not first:
                mix(0, i - 1, ps_y)

        steps = [0]

        def perturb(dst, w, mag, tr, s, done):
            limit = thr[:].rearrange("p s two -> p (s two)").bitcast(F32)

            def done_then(ins):
                steps[0] += 1
                ins.then_inc(tier_step, 1)
                dve.wait_ge(tier_step, steps[0])
            done_then(dve.tensor_scalar(mag.bitcast(U32), w.bitcast(U32), 0x7FFFFFFF, None, ALU.bitwise_and))
            done_then(dve.tensor_scalar(tr, mag, limit[:, s:s + 1], -2.0, ALU.is_ge, ALU.mult))
            done_then(dve.scalar_tensor_tensor(tr, mag, limit[:, s + 1:s + 2], tr, ALU.is_le, ALU.add))
            done_then(dve.tensor_scalar(tr, tr, -1.0, SCALE, ALU.max, ALU.mult))
            dve.scalar_tensor_tensor(dst, tr, 1.0, w, ALU.add, ALU.mult).then_inc(done, 1)

        def last_expert():
            wait(dve, cand_step, sum(BITS) - 1)
            dve.tensor_copy(thr[:, :, 0], prefix[:]).then_inc(thr_ready, 1)
            dve.wait_ge(thr_ready, 2)
            dve.wait_ge(ld_again, 32)
            mag = key[:, 0:2].rearrange("p a n -> p (a n)").bitcast(F32)
            for n in range(2):
                perturb(wagain[:, n, :], wagain[:, n, :], mag, tier, 2 * n, pw_ready)
            dve.wait_ge(pw_ready, 2)
            wait(dve, ex[0]["h_product"], B - 1)
            split([t[:] for t in w1s], wagain[:, 0, :], pw_hi, 1, pw_lo)
            split_x2(0)
            for part, s in ((slice(0, FC), 4), (slice(FC, FC + DC), 6)):
                perturb(bias[:, 1, part], bias[:, 0, part], sabs[:, part], tier[:, part], s, pb_ready)
            wait(dve, ex[0]["y_step"], B - 1)
            split([t[:] for t in w2s], wagain[:, 1, :], pw_hi, 2, pw_lo)
            probabilities(B - 1)
            mix(0, B - 1, ps_s)

        pipeline(dve, body, second_round, last_expert)

        def perturbed_expert(b, first=False):
            s = ex[1]
            if not first:
                split_x2(b)
            for f in range(FC):
                if f == 2 and not first:
                    mix(1, b - 1, ps_m)
                wait(dve, s["g_hi"], b, f + 1)
                wait(dve, s["y_step"], b if f >= 4 else b - 1, f - 3 if f >= 4 else f + 5)
                dve.tensor_tensor(gs[1][:, f % 4, :], g[:, f % 4, :], gs[0][:, f % 4, :].bitcast(F32), ALU.subtract).then_inc(s["g_lo"].handle, 1)

        perturbed_expert(0, first=True)
        with dve.Fori(1, B) as b:
            perturbed_expert(b)
        mix(1, B - 1, ps_m)

    ctx.close()


_INS = ["x", "ctx_1024", "mask_BxSxS2_ff1", "L0_xattn_WQ", "L0_xattn_bQ", "L0_xattn_WK", "L0_xattn_bK",
        "L0_xattn_WV", "L0_xattn_bV", "L0_xattn_Wp", "L0_xattn_bp", "L0_ffn_W1", "L0_ffn_b1", "L0_ffn_W2",
        "L0_ffn_b2", "L0_ffn_ln_gamma", "L0_ffn_ln_beta", "L0_ffn_Wr", "L0_ffn_br"]


def kernel(**inputs):
    import numpy as np
    import concourse.bacc as bacc
    from concourse.bass_utils import run_bass_kernel_spmd

    nc = bacc.Bacc("TRN2", target_bir_lowering=False, num_devices=1)
    arrays, args = {}, []
    for name in _INS:
        a = np.ascontiguousarray(inputs[name])
        arrays["in_" + name] = a
        args.append(nc.dram_tensor("in_" + name, a.shape, mybir.dt.from_np(a.dtype), kind="ExternalInput").ap())
    args.append(nc.dram_tensor("out_x", inputs["x"].shape, F32, kind="ExternalOutput").ap())
    build_program(nc, *args)
    return run_bass_kernel_spmd(nc, [arrays], core_ids=[0]).results[0]["out_x"]
```
